# Optimizing a Trainium2 kernel written in Bass

```python
import numpy as np
import jax
import jax.numpy as jnp

def _softmax(x, axis=-1):
    return jax.nn.softmax(x, axis=axis)

def _gelu(x):
    return jax.nn.gelu(x, approximate=True)

def _silu(x):
    return jax.nn.silu(x)

def _sigmoid(x):
    return jax.nn.sigmoid(x)

def _layernorm(x, axis=-1, eps=1e-05):
    m = jnp.mean(x, axis=axis, keepdims=True)
    v = jnp.var(x, axis=axis, keepdims=True)
    return (x - m) / jnp.sqrt(v + eps)

def _scatter_add(tgt, idx, src, axis=0):
    return tgt.at[idx].add(src)

def _segment_sum(src, seg, n):
    return jax.ops.segment_sum(src, seg, n)
kernel_name = 'mk_xattn_ffn_d1_seqx_r8_e52e14'

def setup_inputs(seed: int=0):
    np.random.seed(seed)
    _w = jnp.asarray

    def _rec_inputs():
        import jax
        import jax.numpy as jnp
        _rk = jax.random.key(seed)
        x = -9.806e-05 + 1 * jax.random.normal(jax.random.fold_in(_rk, 1), (32, 56, 128), jnp.float32)
        _lenS = 56 - jax.random.randint(jax.random.fold_in(_rk, 7), (32,), 0, max(1, 56 // 4) + 1, jnp.int32)
        _lenS2 = 1500 - jax.random.randint(jax.random.fold_in(_rk, 8), (32,), 0, max(1, 1500 // 4) + 1, jnp.int32)
        _ctx_1024P = jax.random.normal(jax.random.fold_in(_rk, 11), (32, 16, 128), jnp.float32)
        _ctx_1024c = jax.random.dirichlet(jax.random.fold_in(_rk, 511), 0.3 * jnp.ones((16,), jnp.float32), (32, 1500))
        _ctx_1024t = jnp.einsum('bsk,bkd->bsd', _ctx_1024c, _ctx_1024P)
        _ctx_1024t = _ctx_1024t * jax.lax.rsqrt(jnp.mean(jnp.square(_ctx_1024t)) + 1e-12) * 0.953939
        ctx_1024 = -1.52775e-05 + 0.999936 * (_ctx_1024t + 0.3 * jax.random.normal(jax.random.fold_in(_rk, 611), (32, 1500, 128), jnp.float32))
        return (x, ctx_1024)
    x, ctx_1024 = _rec_inputs()

    def _L0_xattn_setup():
        import jax, jax.numpy as jnp
        import numpy as np
        D = 128
        NUM_ITERS = 3
        EPS = 1e-06
        SCALE = D ** (-0.5)

        def rmsnorm(x, w, eps=EPS):
            return x * jax.lax.rsqrt(jnp.mean(x * x, axis=-1, keepdims=True) + eps) * w

        def gru_cell(x, h, wih, whh, bih, bhh):
            gx = x @ wih.T + bih
            gh = h @ whh.T + bhh
            xr, xz, xn = jnp.split(gx, 3, axis=-1)
            hr, hz, hn = jnp.split(gh, 3, axis=-1)
            r = jax.nn.sigmoid(xr + hr)
            z = jax.nn.sigmoid(xz + hz)
            n = jnp.tanh(xn + r * hn)
            return (1.0 - z) * n + z * h
        key = jax.random.key(seed)
        ks = jax.random.split(key, 8)
        B, K, M, d = (8, 64, 512, D)
        w_std = d ** (-0.5)
        return {'slots': jax.random.normal(ks[0], (B, K, d), jnp.float32), 'P': jax.random.normal(ks[1], (B, M, d), jnp.float32), 'Wq': jax.random.normal(ks[2], (d, d), jnp.float32) * w_std, 'Wk': jax.random.normal(ks[3], (d, d), jnp.float32) * w_std, 'Wv': jax.random.normal(ks[4], (d, d), jnp.float32) * w_std, 'gru_wih': jax.random.normal(ks[5], (3 * d, d), jnp.float32) * w_std, 'gru_whh': jax.random.normal(ks[6], (3 * d, d), jnp.float32) * w_std, 'gru_bih': jnp.zeros((3 * d,), jnp.float32), 'gru_bhh': jnp.zeros((3 * d,), jnp.float32), 'slot_norm_w': jnp.ones((d,), jnp.float32), 'input_norm_w': jnp.ones((d,), jnp.float32)}
    _L0_xattn_all = _L0_xattn_setup()
    _L0_xattn_in = {k: v for k, v in _L0_xattn_all.items() if k in ('Wq', 'Wk', 'Wv', 'gru_wih', 'gru_whh', 'gru_bih', 'gru_bhh', 'slot_norm_w', 'input_norm_w')}
    del _L0_xattn_all

    def _L0_ffn_setup():
        import jax, jax.numpy as jnp
        import numpy as np
        B, S, D, E, K = (4, 256, 128, 8, 2)
        H = 4 * D
        key = jax.random.key(seed)
        k0, k1, k2, k3 = jax.random.split(key, 4)
        x = jax.random.normal(k0, (B, S, D), dtype=jnp.float32)
        router_w = jax.random.normal(k1, (E, D), dtype=jnp.float32) * 0.02
        w1 = jax.random.normal(k2, (E, H, D), dtype=jnp.float32) * 0.02
        w2 = jax.random.normal(k3, (E, D, H), dtype=jnp.float32) * 0.02
        return {'x': x, 'router_w': router_w, 'w1': w1, 'w2': w2}
    _L0_ffn_all = _L0_ffn_setup()
    _L0_ffn_in = {k: v for k, v in _L0_ffn_all.items() if k in ('router_w', 'w1', 'w2')}
    del _L0_ffn_all
    return {'x': x, 'ctx_1024': ctx_1024, 'L0_xattn_Wq': _L0_xattn_in['Wq'], 'L0_xattn_Wk': _L0_xattn_in['Wk'], 'L0_xattn_Wv': _L0_xattn_in['Wv'], 'L0_xattn_gru_wih': _L0_xattn_in['gru_wih'], 'L0_xattn_gru_whh': _L0_xattn_in['gru_whh'], 'L0_xattn_gru_bih': _L0_xattn_in['gru_bih'], 'L0_xattn_gru_bhh': _L0_xattn_in['gru_bhh'], 'L0_xattn_slot_norm_w': _L0_xattn_in['slot_norm_w'], 'L0_xattn_input_norm_w': _L0_xattn_in['input_norm_w'], 'L0_ffn_router_w': _L0_ffn_in['router_w'], 'L0_ffn_w1': _L0_ffn_in['w1'], 'L0_ffn_w2': _L0_ffn_in['w2']}

def reference(x, ctx_1024, L0_xattn_Wq, L0_xattn_Wk, L0_xattn_Wv, L0_xattn_gru_wih, L0_xattn_gru_whh, L0_xattn_gru_bih, L0_xattn_gru_bhh, L0_xattn_slot_norm_w, L0_xattn_input_norm_w, L0_ffn_router_w, L0_ffn_w1, L0_ffn_w2):
    import jax
    import jax.numpy as jnp

    def _L0_xattn_ref(slots, P, Wq, Wk, Wv, gru_wih, gru_whh, gru_bih, gru_bhh, slot_norm_w, input_norm_w):
        import jax, jax.numpy as jnp
        import numpy as np
        D = 128
        NUM_ITERS = 3
        EPS = 1e-06
        SCALE = D ** (-0.5)

        def rmsnorm(x, w, eps=EPS):
            return x * jax.lax.rsqrt(jnp.mean(x * x, axis=-1, keepdims=True) + eps) * w

        def gru_cell(x, h, wih, whh, bih, bhh):
            gx = x @ wih.T + bih
            gh = h @ whh.T + bhh
            xr, xz, xn = jnp.split(gx, 3, axis=-1)
            hr, hz, hn = jnp.split(gh, 3, axis=-1)
            r = jax.nn.sigmoid(xr + hr)
            z = jax.nn.sigmoid(xz + hz)
            n = jnp.tanh(xn + r * hn)
            return (1.0 - z) * n + z * h
        Pn = rmsnorm(P, input_norm_w)
        k_proj = Pn @ Wk.T
        v_proj = Pn @ Wv.T
        for _ in range(NUM_ITERS):
            sn = rmsnorm(slots, slot_norm_w)
            q_proj = sn @ Wq.T
            scores = jnp.einsum('bkd,bmd->bkm', q_proj, k_proj) * SCALE
            attn = jax.nn.softmax(scores, axis=-2)
            attn = attn / (jnp.sum(attn, axis=-1, keepdims=True) + EPS)
            updates = jnp.einsum('bkm,bmd->bkd', attn, v_proj)
            slots = gru_cell(updates, slots, gru_wih, gru_whh, gru_bih, gru_bhh)
        return slots

    def _L0_ffn_ref(x, router_w, w1, w2):
        import jax, jax.numpy as jnp
        import numpy as np
        B, S, D, E, K = (4, 256, 128, 8, 2)
        H = 4 * D
        b, s, d = x.shape
        e = router_w.shape[0]
        logits = jnp.einsum('bsd,ed->bse', x, router_w)
        probs = jax.nn.softmax(logits, axis=-1)
        topk_vals, topk_idx = jax.lax.top_k(probs, K)
        x_flat = x.reshape(b * s, d)
        vals = topk_vals.reshape(b * s, K)
        idx = topk_idx.reshape(b * s, K)
        out = jnp.zeros_like(x_flat)
        for eid in range(e):
            w = jnp.sum(jnp.where(idx == eid, vals, jnp.zeros((), x.dtype)), axis=-1)
            h = jax.nn.gelu(x_flat @ w1[eid].T, approximate=False)
            y = h @ w2[eid].T
            out = out + w[:, None] * y
        return out.reshape(b, s, d)
    x = x + _L0_xattn_ref(_layernorm(x, axis=-1), ctx_1024, L0_xattn_Wq, L0_xattn_Wk, L0_xattn_Wv, L0_xattn_gru_wih, L0_xattn_gru_whh, L0_xattn_gru_bih, L0_xattn_gru_bhh, L0_xattn_slot_norm_w, L0_xattn_input_norm_w)
    x = x + _L0_ffn_ref(_layernorm(x, axis=-1), L0_ffn_router_w, L0_ffn_w1, L0_ffn_w2)
    return x

_drawn_inputs = setup_inputs


def setup_inputs(seed=0):
    import zlib

    import numpy as np

    out = dict(_drawn_inputs(seed))
    spreads = {'L0_xattn_gru_bih': (0.0, 0.1),
     'L0_xattn_gru_bhh': (0.0, 0.1),
     'L0_xattn_slot_norm_w': (1.0, 0.6),
     'L0_xattn_input_norm_w': (1.0, 0.2)}
    factors = {'L0_ffn_router_w': 6.592, 'L0_ffn_w1': 5.789, 'L0_ffn_w2': 5.736}
    for name, (base, spread) in spreads.items():
        noise = np.random.default_rng([zlib.crc32(name.encode()), seed]).standard_normal(out[name].shape)
        drawn = base * np.exp(spread * noise) if base else spread * noise
        out[name] = jnp.asarray(drawn.astype(out[name].dtype))
    for name, factor in factors.items():
        out[name] = (out[name] * factor).astype(out[name].dtype)
    return out
```

```python
from contextlib import ExitStack

import concourse.bass as bass
from concourse import mybir
from concourse.alu_op_type import AluOpType as ALU

ACT = mybir.ActivationFunctionType
F32 = mybir.dt.float32
AX_X = mybir.AxisListType.X

BATCH, SLOTS, D = 32, 56, 128
TOKENS = 1500
TP = 125
CHUNKS = TOKENS // TP
HALF = CHUNKS // 2
ITERS = 3
PAIR = 8
NPAIR = BATCH // PAIR
GROUP = PAIR // 2
GW = GROUP * SLOTS
PW = PAIR * SLOTS
ROWS = 2 * SLOTS
RT = PW // ROWS
STEPS = ITERS * PAIR
GSTEPS = ITERS * 2
PTILES = 3
PTW = TOKENS // PTILES
CPT = CHUNKS // PTILES
EXPERTS, HIDDEN = 8, 512
HC = HIDDEN // D
WTILES = EXPERTS
SCALE = float(D) ** -0.5
EPS_RMS, EPS_ATTN, EPS_LN = 1e-6, 1e-6, 1e-5
DMA = 16
XDMA_ROWS = 112


def slot_attention_moe(nc, x, ctx, wq, wk, wv, wih, whh, bih, bhh, slot_w, input_w, router, w1, w2, out):
    with ExitStack() as stack:
        def sb(name, shape, dt=F32):
            return stack.enter_context(nc.sbuf_tensor(name, shape, dt))

        def psum(name, shape):
            return stack.enter_context(nc.psum_tensor(name, shape, F32))

        def sem(name):
            return stack.enter_context(nc.semaphore(name))

        ctx_rows = sb("ctx_rows", [128, PAIR, CHUNKS, D])
        ctx_cols = sb("ctx_cols", [128, PAIR, TOKENS])
        square = sb("square", [128, 2, CHUNKS, D])
        ssq = sb("ssq", [128, 2, CHUNKS])
        ctx_ms = sb("ctx_ms", [128, 2, CHUNKS])
        ctx_rstd = sb("ctx_rstd", [128, 2, CHUNKS])
        shifted = sb("shifted", [128, 2, CHUNKS, SLOTS])
        attn = sb("attn", [128, 4, CHUNKS, SLOTS])
        top = sb("top", [128, 2, CHUNKS])
        den = sb("den", [128, 2, CHUNKS])
        rden = sb("rden", [128, 2, CHUNKS])
        h = sb("h", [128, 2, GW])
        qk = sb("qk", [128, 2, GW])
        h_sq = sb("h_sq", [128, GW])
        ln_ms = sb("ln_ms", [128, GW])
        h_rstd = sb("h_rstd", [128, GW])
        inv_sum = sb("inv_sum", [128, GW])
        upd = sb("upd", [128, GW])
        gates = sb("gates", [128, 2 * GW])
        npre = sb("npre", [128, GW])
        nexp = sb("nexp", [128, GW])
        cand = sb("cand", [128, GW])
        diff = sb("diff", [128, GW])
        x_in = sb("x_in", [ROWS, RT, D])
        acc = sb("acc", [ROWS, RT, D])
        normed = sb("normed", [ROWS, RT, D])
        stats = sb("stats", [ROWS, RT, 6])
        mv = sb("mv", [ROWS, RT, 2])
        row_var = sb("row_var", [ROWS, RT])
        row_rstd = sb("row_rstd", [ROWS, RT])
        ycols = sb("ycols", [128, PW])
        hidden = sb("hidden", [128, 2, HC, PW])
        w1_t = sb("w1_t", [128, EXPERTS, HIDDEN])
        w2_t = sb("w2_t", [128, EXPERTS, HC, D])
        stage = sb("stage", [128, 2, HC, D])
        router_raw = sb("router_raw", [EXPERTS, D])
        router_t = sb("router_t", [128, EXPERTS])
        wq_sb = sb("wq_sb", [128, D])
        wk_sb = sb("wk_sb", [128, D])
        wv_sb = sb("wv_sb", [128, D])
        gru_raw = sb("gru_raw", [128, 6, D])
        wih_t = sb("wih_t", [128, 3 * D])
        wx_t = sb("wx_t", [128, 3 * D])
        wh_t = sb("wh_t", [128, 3 * D])
        wqk = sb("wqk", [128, D])
        vec_raw = sb("vec_raw", [8, D])
        vec = sb("vec", [128, 8])
        key_scale = sb("key_scale", [128, 1])
        value_scale = sb("value_scale", [128, 1])
        neg_rz = sb("neg_rz", [128, 2])
        neg_2bn = sb("neg_2bn", [128, 1])
        ident = sb("ident", [128, 128])
        ones = sb("ones", [128, 128])
        eps_col = sb("eps_col", [128, 1])
        ssq_eps = sb("ssq_eps", [128, CHUNKS])
        var_eps = sb("var_eps", [ROWS, RT])
        spare = sb("spare", [128, 1])
        mhalf = sb("mhalf", [128, CHUNKS])
        rank = sb("rank", [ROWS, RT, EXPERTS])
        rs_z = sb("rs_z", [ROWS, RT, EXPERTS])
        rs_e = sb("rs_e", [ROWS, RT, EXPERTS])
        rs_p = sb("rs_p", [ROWS, RT, EXPERTS])
        rs_k = sb("rs_k", [ROWS, RT, EXPERTS])
        rs_1 = sb("rs_1", [ROWS, RT, EXPERTS])
        rs_q = sb("rs_q", [ROWS, RT, EXPERTS])
        rs_m = sb("rs_m", [ROWS, RT])
        mix = sb("mix", [ROWS, RT, EXPERTS])

        score_ps = psum("score_ps", [128, 4, 512])
        upd_ps = psum("upd_ps", [128, 2, 512])
        gru_ps = psum("gru_ps", [128, 2, 512])

        consts_ready = sem("consts_ready")
        wq_loaded, wk_loaded, wv_loaded = sem("wq_loaded"), sem("wk_loaded"), sem("wv_loaded")
        vec_loaded, gruw_loaded, router_loaded = sem("vec_loaded"), sem("gruw_loaded"), sem("router_loaded")
        stage_loaded = [sem("stage_loaded0"), sem("stage_loaded1")]
        ctx_loaded = [sem(f"ctx_loaded{b}") for b in range(PAIR)]
        x_loaded, out_stored = sem("x_loaded"), sem("out_stored")
        setup_mm, setup_copied = sem("setup_mm"), sem("setup_copied")
        wtile_turned, wtile_copied = sem("wtile_turned"), sem("wtile_copied")
        squared, ssq_ready, ctx_scaled = sem("squared"), sem("ssq_ready"), sem("ctx_scaled")
        ctx_turned, ctx_copied = sem("ctx_turned"), sem("ctx_copied")
        scores_ready, max_ready, shift_ready = sem("scores_ready"), sem("max_ready"), sem("shift_ready")
        exp_ready, den_ready, rden_ready = sem("exp_ready"), sem("den_ready"), sem("rden_ready")
        attn_ready, upd_ready, upd_normed = sem("attn_ready"), sem("upd_ready"), sem("upd_normed")
        gates_mm, gates_exp, npre_ready = sem("gates_mm"), sem("gates_exp"), sem("npre_ready")
        nexp_ready, cand_ready, h_ready = sem("nexp_ready"), sem("cand_ready"), sem("h_ready")
        h_squared, q_mm, h_rstd_ready, qk_ready = sem("h_squared"), sem("q_mm"), sem("h_rstd_ready"), sem("qk_ready")
        h_turned, x1_ready, var_ready, rstd_ready = sem("h_turned"), sem("x1_ready"), sem("var_ready"), sem("rstd_ready")
        normed_ready, normed_turned, cols_ready = sem("normed_ready"), sem("normed_turned"), sem("cols_ready")
        logits_ready, router_shift, router_exp = sem("logits_ready"), sem("router_shift"), sem("router_exp")
        up_ready, gelu_ready, down_ready, mixed = sem("up_ready"), sem("gelu_ready"), sem("down_ready"), sem("mixed")
        dve_order, act_order, pool_order = sem("dve_order"), sem("act_order"), sem("pool_order")

        LN_PER = 2

        def nth(i, per, n):
            return i * per + n

        def wait(eng, semaphore, value):
            eng.wait_ge(semaphore, value)

        def wait_reuse(eng, semaphore, i, per, n):
            if n >= 1:
                eng.wait_ge(semaphore, nth(i, per, n))

        class Chain:
            def __init__(self, eng, semaphore):
                self.eng, self.semaphore, self.base, self.count = eng, semaphore, 0, 0

            def enter(self, base):
                self.base, self.count = base, 0

            def link(self, ins):
                self.count += 1
                ins.then_inc(self.semaphore, 1)
                self.eng.wait_ge(self.semaphore, self.base + self.count)

        def batch_of(i, b):
            return i * PAIR + b

        block = stack.enter_context(nc.Block())

        @block.sync
        def _(sp):
            def load_ctx(j, b):
                src = ctx[batch_of(j, b):batch_of(j, b) + 1] if isinstance(j, int) else ctx[bass.ds(batch_of(j, b), 1)]
                src = src.rearrange("o (p c) d -> p (o c) d", c=CHUNKS)
                sp.dma_start(ctx_rows[0:XDMA_ROWS, b], src[0:XDMA_ROWS]).then_inc(ctx_loaded[b], DMA)
                sp.dma_start(ctx_rows[XDMA_ROWS:TP, b], src[XDMA_ROWS:TP]).then_inc(ctx_loaded[b], DMA)

            def rows_of(t, j):
                j8 = t[j * PAIR:(j + 1) * PAIR] if isinstance(j, int) else t[bass.ds(j * PAIR, PAIR)]
                return j8.rearrange("(t b) k d -> (b k) t d", b=2)

            sp.dma_start(wq_sb[:], wq).then_inc(wq_loaded, DMA)
            sp.dma_start(wk_sb[:], wk).then_inc(wk_loaded, DMA)
            sp.dma_start(vec_raw[0:3, :], bih.rearrange("(g d) -> g d", d=D)).then_inc(vec_loaded, DMA)
            sp.dma_start(vec_raw[3:6, :], bhh.rearrange("(g d) -> g d", d=D)).then_inc(vec_loaded, DMA)
            sp.dma_start(vec_raw[6:7, :], slot_w.rearrange("(g d) -> g d", d=D)).then_inc(vec_loaded, DMA)
            sp.dma_start(vec_raw[7:8, :], input_w.rearrange("(g d) -> g d", d=D)).then_inc(vec_loaded, DMA)
            sp.dma_start(x_in[:], rows_of(x, 0)).then_inc(x_loaded, DMA)
            load_ctx(0, 0)
            sp.dma_start(wv_sb[:], wv).then_inc(wv_loaded, DMA)
            sp.dma_start(gru_raw[:, 0:3, :], wih.rearrange("(g p) d -> p g d", p=128)).then_inc(gruw_loaded, DMA)
            sp.dma_start(gru_raw[:, 3:6, :], whh.rearrange("(g p) d -> p g d", p=128)).then_inc(gruw_loaded, DMA)
            sp.dma_start(router_raw[:], router).then_inc(router_loaded, DMA)
            for b in range(1, PAIR):
                load_ctx(0, b)
            for t in range(2 * WTILES):
                if t >= 2:
                    sp.wait_ge(wtile_turned, t - 1)
                if t < WTILES:
                    src = w1[t].rearrange("(c p) d -> p c d", p=128)
                else:
                    src = w2[t - WTILES].rearrange("d (c p) -> d c p", p=128)
                sp.dma_start(stage[:, t % 2], src).then_inc(stage_loaded[t % 2], DMA)

            def body(i, more):
                if more:
                    for b in range(PAIR):
                        wait(sp, upd_ready, nth(i, STEPS, STEPS - PAIR + b + 1))
                        load_ctx(i + 1, b)
                    wait(sp, x1_ready, nth(i, 1, 1))
                    sp.dma_start(x_in[:], rows_of(x, i + 1)).then_inc(x_loaded, DMA)
                wait(sp, mixed, nth(i, EXPERTS, EXPERTS))
                sp.dma_start(rows_of(out, i), acc[:]).then_inc(out_stored, DMA)

            with sp.Fori(0, NPAIR - 1) as i:
                body(i, True)
            body(NPAIR - 1, False)
            sp.wait_ge(out_stored, DMA * (NPAIR + 1))

        @block.tensor
        def _(pe):
            def turn_ctx(j, b):
                wait(pe, ctx_scaled, nth(j, PAIR, b + 1))
                for t in range(PTILES):
                    n = PTILES * b + t
                    wait_reuse(pe, ctx_copied, j, PTILES * PAIR, n - 1)
                    for c in range(CPT):
                        mm = pe.transpose(upd_ps[:, n % 2, c * TP:(c + 1) * TP],
                                          ctx_rows[0:TP, b, t * CPT + c, :], ident[0:TP, 0:TP])
                    mm.then_inc(ctx_turned, 1)

            def turn_normed(n):
                wait(pe, normed_ready, n)
                for t in range(RT):
                    mm = pe.transpose(gru_ps[:, 1, t * ROWS:(t + 1) * ROWS], normed[:, t, :],
                                      ident[0:ROWS, 0:ROWS])
                mm.then_inc(normed_turned, 1)

            def queries(i, n, g):
                wait(pe, h_squared, nth(i, GSTEPS, n + 1))
                pe.matmul(gru_ps[:, 0, 0:GW], ones[:, :], h_sq[:, :], start=True, stop=True)
                pe.matmul(gru_ps[:, 0, GW:2 * GW], wqk[:, :], h[:, g, :], start=True, stop=True).then_inc(q_mm, 1)

            def scores(i, s):
                b, g = s % PAIR, (s % PAIR) // GROUP
                if s % GROUP == 0:
                    wait(pe, qk_ready, nth(i, GSTEPS, s // GROUP + 1))
                if s < PAIR:
                    wait(pe, ctx_copied, nth(i, PTILES * PAIR, PTILES * (b + 1)))
                wait_reuse(pe, shift_ready, i, STEPS, s - 1)
                for c in range(CHUNKS):
                    o = (c % HALF) * SLOTS
                    mm = pe.matmul(score_ps[0:TP, 2 * (s % 2) + c // HALF, o:o + SLOTS],
                                   ctx_cols[:, b, c * TP:(c + 1) * TP],
                                   qk[:, g, (b % GROUP) * SLOTS:(b % GROUP + 1) * SLOTS], start=True, stop=True)
                mm.then_inc(scores_ready, 1)

            def update(i, s):
                b, gs = s % PAIR, s // GROUP
                wait(pe, attn_ready, nth(i, STEPS, s + 1))
                if s % GROUP == 0:
                    wait_reuse(pe, upd_normed, i, GSTEPS, gs - 1)
                o = (b % GROUP) * SLOTS
                for c in range(CHUNKS):
                    pe.matmul(upd_ps[:, gs % 2, o:o + SLOTS], ctx_rows[0:TP, b, c, :], attn[0:TP, s % 4, c, :],
                              start=(c == 0), stop=(c == CHUNKS - 1))
                for c in range(CHUNKS):
                    mm = pe.matmul(upd_ps[:, gs % 2, GW + o:GW + o + SLOTS], ones[0:TP, :], attn[0:TP, s % 4, c, :],
                                   start=(c == 0), stop=(c == CHUNKS - 1))
                mm.then_inc(upd_ready, 1)

            def gate_products(i, gs):
                g = gs % 2
                wait(pe, upd_normed, nth(i, GSTEPS, gs + 1))
                for part in range(2):
                    o = part * GW
                    pe.matmul(gru_ps[:, 0, o:o + GW], wx_t[:, part * D:(part + 1) * D], upd[:, :],
                              start=True, stop=False)
                    pe.matmul(gru_ps[:, 0, o:o + GW], wh_t[:, part * D:(part + 1) * D], h[:, g, :],
                              start=False, stop=True)
                pe.matmul(gru_ps[:, 1, 0:GW], wx_t[:, 2 * D:3 * D], upd[:, :], start=True, stop=True)
                pe.matmul(gru_ps[:, 1, GW:2 * GW], wh_t[:, 2 * D:3 * D], h[:, g, :],
                          start=True, stop=True).then_inc(gates_mm, 1)

            def up(i, e):
                for c in range(HC):
                    n = HC * e + c
                    wait_reuse(pe, gelu_ready, i, EXPERTS * HC, n - 1)
                    pe.matmul(score_ps[:, n % 2, 0:PW], w1_t[:, e, c * D:(c + 1) * D], ycols[:, :],
                              start=True, stop=True).then_inc(up_ready, 1)

            def down(i, e):
                wait(pe, gelu_ready, nth(i, EXPERTS * HC, HC * (e + 1)))
                wait_reuse(pe, mixed, i, EXPERTS, e - 1)
                for t in range(RT):
                    for c in range(HC):
                        mm = pe.matmul(score_ps[0:ROWS, 2 + e % 2, t * D:(t + 1) * D],
                                       hidden[:, e % 2, c, t * ROWS:(t + 1) * ROWS], w2_t[:, e, c, :],
                                       start=(c == 0), stop=(c == HC - 1))
                mm.then_inc(down_ready, 1)

            pe.wait_ge(consts_ready, 1)
            pe.wait_ge(vec_loaded, 4 * DMA)
            pe.transpose(gru_ps[:, 0, 0:8], vec_raw[:, :], ident[0:8, 0:8]).then_inc(setup_mm, 1)
            pe.wait_ge(wq_loaded, DMA)
            pe.wait_ge(wk_loaded, DMA)
            pe.matmul(score_ps[:, 0, 0:D], wq_sb[:, :], wk_sb[:, :], start=True, stop=True).then_inc(setup_mm, 1)
            turn_normed(1)
            pe.wait_ge(gruw_loaded, 2 * DMA)
            for side in range(2):
                for g in range(3):
                    mm = pe.transpose(score_ps[:, 1 + side, g * D:(g + 1) * D], gru_raw[:, 3 * side + g, :], ident[:, :])
                mm.then_inc(setup_mm, 1)
            pe.wait_ge(router_loaded, DMA)
            pe.transpose(score_ps[:, 3, 0:EXPERTS], router_raw[:, :], ident[0:EXPERTS, 0:EXPERTS]).then_inc(setup_mm, 1)
            pe.wait_ge(wv_loaded, DMA)
            pe.wait_ge(setup_copied, 5)
            pe.matmul(score_ps[:, 0, 0:3 * D], wv_sb[:, :], wih_t[:, :], start=True, stop=True).then_inc(setup_mm, 1)
            for b in range(PAIR):
                turn_ctx(0, b)
            pe.wait_ge(setup_copied, 6)
            for t in range(2 * WTILES):
                pe.wait_ge(stage_loaded[t % 2], DMA * (t // 2 + 1))
                if t >= 4:
                    pe.wait_ge(wtile_copied, t - 3)
                for c in range(HC):
                    mm = pe.transpose(score_ps[:, t % 4, c * D:(c + 1) * D], stage[:, t % 2, c, :], ident[:, :])
                mm.then_inc(wtile_turned, 1)

            def body(i, more):
                wait(pe, cols_ready, nth(i, LN_PER, 1))
                queries(i, 0, 0)
                wait(pe, qk_ready, nth(i, GSTEPS, 1))
                queries(i, 1, 1)
                for n in range(STEPS + 4):
                    gs, phase = divmod(n - 6, GROUP)
                    if n < STEPS:
                        scores(i, n)
                    if gs >= 0 and phase == 0:
                        gate_products(i, gs)
                    if 2 <= n < STEPS + 2:
                        update(i, n - 2)
                    if gs >= 0 and phase == 1 and gs < GSTEPS - 2:
                        queries(i, gs + 2, gs % 2)
                wait(pe, h_ready, nth(i, GSTEPS, GSTEPS))
                for t in range(RT):
                    cols = h[:, :, :].rearrange("p g w -> p (g w)")[:, t * ROWS:(t + 1) * ROWS]
                    mm = pe.transpose(gru_ps[0:ROWS, 0, t * D:(t + 1) * D], cols, ident[:, :])
                mm.then_inc(h_turned, 1)
                turn_normed(nth(i, LN_PER, 2))
                wait(pe, cols_ready, nth(i, LN_PER, 2))
                for t in range(RT):
                    mm = pe.matmul(gru_ps[0:ROWS, 0, t * EXPERTS:(t + 1) * EXPERTS],
                                   ycols[:, t * ROWS:(t + 1) * ROWS], router_t[:, :], start=True, stop=True)
                mm.then_inc(logits_ready, 1)
                if not isinstance(i, int) or i == 0:
                    pe.wait_ge(wtile_copied, 2 * WTILES)
                for e in range(EXPERTS):
                    up(i, e)
                    if e >= 1:
                        down(i, e - 1)
                        if more:
                            turn_ctx(i + 1, e - 1)
                    if more and e == 4:
                        turn_normed(nth(i + 1, LN_PER, 1))
                down(i, EXPERTS - 1)
                if more:
                    turn_ctx(i + 1, EXPERTS - 1)

            with pe.Fori(0, NPAIR - 1) as i:
                body(i, True)
            body(NPAIR - 1, False)

        @block.scalar
        def _(act):
            chain = Chain(act, act_order)
            PER = GSTEPS

            def square_ctx(j, b):
                wait(act, ctx_loaded[b], nth(j, 2 * DMA, 2 * DMA))
                wait_reuse(act, ssq_ready, j, PAIR, b - 1)
                nc.scalar.activation(square[0:TP, b % 2], ctx_rows[0:TP, b], ACT.Square).then_inc(squared, 1)

            def copy_cols(dst, n):
                wait(act, normed_turned, n)
                nc.scalar.copy(dst, gru_ps[:, 1, 0:PW]).then_inc(cols_ready, 1)

            def square_h(i, n, g):
                nc.scalar.activation(h_sq[:, :], h[:, g, :], ACT.Square).then_inc(h_squared, 1)

            def rstd_h(i, n):
                wait(act, q_mm, nth(i, GSTEPS, n + 1))
                chain.link(nc.scalar.activation(ln_ms[:, :], gru_ps[:, 0, 0:GW], ACT.Ln,
                                                bias=eps_col[:, :], scale=1.0 / D))
                nc.scalar.activation(h_rstd[:, :], ln_ms[:, :], ACT.Exp, scale=-0.5).then_inc(h_rstd_ready, 1)

            act.preload_act_table(ACT.Ln)
            hflat = h[:, :, :].rearrange("p g w -> p (g w)")
            copy_cols(hflat, 1)
            for b in range(PAIR):
                square_ctx(0, b)
            for t in range(2 * WTILES):
                act.wait_ge(wtile_turned, t + 1)
                dst = w1_t[:, t, :] if t < WTILES else w2_t[:, t - WTILES].rearrange("p c d -> p (c d)")
                nc.scalar.copy(dst, score_ps[:, t % 4, :]).then_inc(wtile_copied, 1)

            def body(i, more):
                chain.enter(i * PER)
                act.preload_act_table(ACT.Ln)
                wait(act, cols_ready, nth(i, LN_PER, 1))
                for g in range(2):
                    square_h(i, g, g)
                    rstd_h(i, g)
                for n in range(STEPS + 4):
                    gs, phase = divmod(n - 6, GROUP)
                    if gs >= 0 and phase == 1:
                        wait(act, gates_mm, nth(i, GSTEPS, gs + 1))
                        for part in range(2):
                            nc.scalar.activation(gates[:, part * GW:(part + 1) * GW],
                                                 gru_ps[:, 0, part * GW:(part + 1) * GW], ACT.Exp,
                                                 bias=neg_rz[:, part:part + 1], scale=-1.0).then_inc(gates_exp, 1)
                        wait(act, npre_ready, nth(i, GSTEPS, gs + 1))
                        nc.scalar.activation(nexp[:, :], npre[:, :], ACT.Exp, bias=neg_2bn[:, :],
                                             scale=-2.0).then_inc(nexp_ready, 1)
                    if n < STEPS:
                        wait(act, shift_ready, nth(i, STEPS, n + 1))
                        wait_reuse(act, upd_ready, i, STEPS, n - 3)
                        nc.scalar.activation(attn[0:TP, n % 4], shifted[0:TP, n % 2], ACT.Exp).then_inc(exp_ready, 1)
                    if gs >= 0 and phase == 1 and gs < GSTEPS - 2:
                        wait(act, h_ready, nth(i, GSTEPS, gs + 1))
                        square_h(i, gs + 2, gs % 2)
                        rstd_h(i, gs + 2)
                copy_cols(ycols[:, :], nth(i, LN_PER, 2))
                wait(act, router_shift, nth(i, 1, 1))
                nc.scalar.activation(rs_e[:], rs_z[:], ACT.Exp).then_inc(router_exp, 1)
                for e in range(EXPERTS):
                    for c in range(HC):
                        n = HC * e + c
                        wait(act, up_ready, nth(i, EXPERTS * HC, n + 1))
                        if c == 0:
                            wait_reuse(act, down_ready, i, EXPERTS, e - 1)
                        nc.scalar.activation(hidden[:, e % 2, c, :], score_ps[:, n % 2, 0:PW],
                                             ACT.Gelu).then_inc(gelu_ready, 1)
                    if more:
                        square_ctx(i + 1, e)
                        if e == 4:
                            copy_cols(hflat, nth(i + 1, LN_PER, 1))

            with act.Fori(0, NPAIR - 1) as i:
                body(i, True)
            body(NPAIR - 1, False)

        @block.gpsimd
        def _(pool):
            chain = Chain(pool, pool_order)
            GRU_LINKS, CTX_LINKS, LN_LINKS = 2, 2, 1
            PRO = 3 + CTX_LINKS * PAIR + LN_LINKS
            PER = GRU_LINKS * GSTEPS + CTX_LINKS * PAIR + 2 * LN_LINKS

            def scale_ctx(j, b):
                r = b % 2
                wait(pool, ssq_ready, nth(j, PAIR, b + 1))
                chain.link(nc.gpsimd.tensor_tensor(ctx_ms[0:TP, r], ssq[0:TP, r], ssq_eps[0:TP, :], ALU.add))
                chain.link(nc.gpsimd.tensor_tensor(ctx_rstd[0:TP, r], ctx_ms[0:TP, r], mhalf[0:TP, :], ALU.pow))
                rows = ctx_rows[0:TP, b]
                nc.gpsimd.tensor_tensor(rows, rows, ctx_rstd[0:TP, r].unsqueeze(2).to_broadcast([TP, CHUNKS, D]),
                                        ALU.mult).then_inc(ctx_scaled, 1)

            def rstd_rows(n):
                wait(pool, var_ready, n)
                chain.link(nc.gpsimd.tensor_tensor(row_var[:, :], mv[:, :, 1], var_eps[:, :], ALU.add))
                nc.gpsimd.tensor_tensor(row_rstd[:, :], row_var[:, :], mhalf[0:ROWS, 0:RT], ALU.pow).then_inc(rstd_ready, 1)

            chain.link(nc.gpsimd.memset(ones[:, :], 1.0))
            chain.link(nc.gpsimd.affine_select(out=ident[:, :], in_=ones[:, :], compare_op=ALU.is_equal, fill=0.0,
                                               base=0, pattern=[[-1, 128]], channel_multiplier=1))
            nc.gpsimd.memset(eps_col[:, :], EPS_RMS)
            nc.gpsimd.memset(ssq_eps[:, :], D * EPS_RMS)
            nc.gpsimd.memset(var_eps[:, :], EPS_LN)
            for e in range(EXPERTS):
                nc.gpsimd.memset(rank[:, :, e], float(EXPERTS - e))
            chain.link(nc.gpsimd.memset(mhalf[:, :], -0.5))
            nc.gpsimd.memset(h_sq[:, 0:1], 0.0).then_inc(consts_ready, 1)
            rstd_rows(1)
            for b in range(PAIR):
                scale_ctx(0, b)

            def body(i, more):
                chain.enter(PRO + i * PER)
                for n in range(STEPS + 4):
                    gs, phase = divmod(n - 6, GROUP)
                    if gs >= 0 and phase == 1:
                        hg, z = h[:, gs % 2, :], gates[:, GW:2 * GW]
                        wait(pool, cand_ready, nth(i, GSTEPS, gs + 1))
                        chain.link(nc.gpsimd.tensor_tensor(diff[:, :], hg, cand[:, :], ALU.subtract))
                        chain.link(nc.gpsimd.tensor_tensor(diff[:, :], diff[:, :], z, ALU.mult))
                        nc.gpsimd.tensor_tensor(hg, diff[:, :], cand[:, :], ALU.add).then_inc(h_ready, 1)
                    if 1 <= n <= STEPS:
                        s = n - 1
                        wait(pool, rden_ready, nth(i, STEPS, s + 1))
                        a = attn[0:TP, s % 4]
                        nc.gpsimd.tensor_tensor(a, a, rden[0:TP, s % 2].unsqueeze(2).to_broadcast([TP, CHUNKS, SLOTS]),
                                                ALU.mult).then_inc(attn_ready, 1)
                rstd_rows(nth(i, LN_PER, 2))
                if more:
                    for e in range(EXPERTS):
                        scale_ctx(i + 1, e)
                        if e == 3:
                            rstd_rows(nth(i + 1, LN_PER, 1))

            with pool.Fori(0, NPAIR - 1) as i:
                body(i, True)
            body(NPAIR - 1, False)

        @block.vector
        def _(dve):
            chain = Chain(dve, dve_order)
            LN_LINKS, GRU_LINKS, ROUTER_LINKS = 1, 7, 17
            PRO = 1 + LN_LINKS
            PER = 2 * LN_LINKS + GRU_LINKS * GSTEPS + ROUTER_LINKS

            def sum_squares(j, b):
                wait(dve, squared, nth(j, PAIR, b + 1))
                wait_reuse(dve, ctx_scaled, j, PAIR, b - 1)
                nc.vector.tensor_reduce(ssq[0:TP, b % 2], square[0:TP, b % 2], AX_X, ALU.add).then_inc(ssq_ready, 1)

            def copy_ctx(j, b):
                for t in range(PTILES):
                    n = PTILES * b + t
                    wait(dve, ctx_turned, nth(j, PTILES * PAIR, n + 1))
                    nc.vector.tensor_copy(ctx_cols[:, b, t * PTW:(t + 1) * PTW], upd_ps[:, n % 2, 0:PTW])\
                        .then_inc(ctx_copied, 1)

            def layernorm(src, n):
                for t in range(RT):
                    ins = nc.vector.bn_stats(stats[:, t, :], src[:, t, :])
                chain.link(ins)
                nc.vector.memset(spare[:, :], 0.0)
                for t in range(RT):
                    ins = nc.vector.bn_aggr(mv[:, t, :], stats[:, t, :])
                ins.then_inc(var_ready, 1)
                wait(dve, rstd_ready, n)
                for t in range(RT):
                    ins = nc.vector.tensor_scalar(normed[:, t, :], src[:, t, :], mv[:, t, 0:1], row_rstd[:, t:t + 1],
                                                  ALU.subtract, ALU.mult)
                ins.then_inc(normed_ready, 1)

            def make_qk(i, n, g):
                wait(dve, h_rstd_ready, nth(i, GSTEPS, n + 1))
                nc.vector.scalar_tensor_tensor(out=qk[:, g, :], in0=gru_ps[:, 0, GW:2 * GW], scalar=key_scale[:, :],
                                               in1=h_rstd[:, :], op0=ALU.mult, op1=ALU.mult).then_inc(qk_ready, 1)

            dve.sem_inc(out_stored, DMA)
            dve.wait_ge(setup_mm, 1)
            chain.link(nc.vector.tensor_copy(vec[:, :], gru_ps[:, 0, 0:8]))
            nc.vector.tensor_scalar(key_scale[:, :], vec[:, 7:8], SCALE * D ** 0.5, None, ALU.mult)
            nc.vector.tensor_scalar(value_scale[:, :], vec[:, 7:8], D ** 0.5, None, ALU.mult)
            nc.vector.scalar_tensor_tensor(out=neg_rz[:, :], in0=vec[:, 0:2], scalar=-1.0, in1=vec[:, 3:5],
                                           op0=ALU.mult, op1=ALU.subtract)
            nc.vector.tensor_scalar(neg_2bn[:, :], vec[:, 2:3], -2.0, None, ALU.mult).then_inc(setup_copied, 1)
            dve.wait_ge(setup_mm, 2)
            nc.vector.tensor_scalar(wqk[:, :], score_ps[:, 0, 0:D], vec[:, 6:7], None, ALU.mult).then_inc(setup_copied, 1)
            dve.wait_ge(x_loaded, DMA)
            layernorm(x_in, 1)
            dve.wait_ge(setup_mm, 3)
            nc.vector.tensor_copy(wih_t[:, :], score_ps[:, 1, 0:3 * D]).then_inc(setup_copied, 1)
            dve.wait_ge(setup_mm, 4)
            nc.vector.tensor_copy(wh_t[:, :], score_ps[:, 2, 0:3 * D]).then_inc(setup_copied, 1)
            dve.wait_ge(setup_mm, 5)
            nc.vector.tensor_copy(router_t[:, :], score_ps[:, 3, 0:EXPERTS]).then_inc(setup_copied, 1)
            dve.wait_ge(setup_mm, 6)
            nc.vector.tensor_scalar(wx_t[:, :], score_ps[:, 0, 0:3 * D], value_scale[:, :], None, ALU.mult)\
                .then_inc(setup_copied, 1)
            for b in range(PAIR + 1):
                if b < PAIR:
                    sum_squares(0, b)
                if b >= 1:
                    copy_ctx(0, b - 1)

            def router_weights(i):
                def wide(a):
                    return a.unsqueeze(2).to_broadcast([ROWS, RT, EXPERTS])
                logits = gru_ps[0:ROWS, 0, 0:RT * EXPERTS].rearrange("p (t e) -> p t e", e=EXPERTS)
                wait(dve, logits_ready, nth(i, 1, 1))
                chain.link(nc.vector.tensor_reduce(rs_m[:], logits, AX_X, ALU.max))
                nc.vector.tensor_tensor(rs_z[:], logits, wide(rs_m[:]), ALU.subtract).then_inc(router_shift, 1)
                wait(dve, router_exp, nth(i, 1, 1))
                chain.link(nc.vector.tensor_reduce(rs_m[:], rs_e[:], AX_X, ALU.add))
                chain.link(nc.vector.reciprocal(rs_m[:], rs_m[:]))
                chain.link(nc.vector.tensor_tensor(rs_p[:], rs_e[:], wide(rs_m[:]), ALU.mult))

                def largest(src, dst):
                    chain.link(nc.vector.tensor_reduce(rs_m[:], src[:], AX_X, ALU.max))
                    chain.link(nc.vector.tensor_tensor(rs_k[:], src[:], wide(rs_m[:]), ALU.is_equal))
                    chain.link(nc.vector.tensor_tensor(rs_k[:], rs_k[:], rank[:], ALU.mult))
                    chain.link(nc.vector.tensor_reduce(rs_m[:], rs_k[:], AX_X, ALU.max))
                    chain.link(nc.vector.tensor_tensor(dst[:], rs_k[:], wide(rs_m[:]), ALU.is_equal))

                largest(rs_p, rs_1)
                chain.link(nc.vector.scalar_tensor_tensor(out=rs_q[:], in0=rs_1[:], scalar=-2.0, in1=rs_p[:],
                                                          op0=ALU.mult, op1=ALU.add))
                largest(rs_q, rs_z)
                return rs_1, rs_z

            def body(i, more):
                chain.enter(PRO + i * PER)
                for g in range(2):
                    make_qk(i, g, g)
                for n in range(STEPS + 4):
                    gs, phase = divmod(n - 6, GROUP)
                    if gs >= 0 and phase == 1:
                        wait(dve, gates_exp, nth(i, 2 * GSTEPS, 2 * gs + 2))
                        chain.link(nc.vector.tensor_scalar(gates[:, :], gates[:, :], 1.0, None, ALU.add))
                        chain.link(nc.vector.reciprocal(gates[:, :], gates[:, :]))
                        chain.link(nc.vector.scalar_tensor_tensor(
                            out=npre[:, :], in0=gru_ps[:, 1, GW:2 * GW], scalar=vec[:, 5:6], in1=gates[:, 0:GW],
                            op0=ALU.add, op1=ALU.mult))
                        nc.vector.tensor_tensor(npre[:, :], gru_ps[:, 1, 0:GW], npre[:, :], ALU.add)\
                            .then_inc(npre_ready, 1)
                    if n < STEPS:
                        banks = score_ps[0:TP, 2 * (n % 2):2 * (n % 2) + 2, 0:HALF * SLOTS]\
                            .rearrange("p h (c k) -> p h c k", k=SLOTS)
                        wait(dve, scores_ready, nth(i, STEPS, n + 1))
                        nc.vector.tensor_reduce(top[0:TP, n % 2], banks, AX_X, ALU.max).then_inc(max_ready, 1)
                        wait(dve, max_ready, nth(i, STEPS, n + 1))
                        wait_reuse(dve, exp_ready, i, STEPS, n - 1)
                        tops = top[0:TP, n % 2].rearrange("p (h c) -> p h c", h=2).unsqueeze(3)\
                            .to_broadcast([TP, 2, HALF, SLOTS])
                        nc.vector.tensor_tensor(shifted[0:TP, n % 2].rearrange("p (h c) k -> p h c k", h=2), banks,
                                                tops, ALU.subtract).then_inc(shift_ready, 1)
                    if gs >= 0 and phase == 0:
                        wait(dve, upd_ready, nth(i, STEPS, GROUP * (gs + 1)))
                        chain.link(nc.vector.tensor_scalar(inv_sum[:, :], upd_ps[:, gs % 2, GW:2 * GW], EPS_ATTN, None,
                                                           ALU.add))
                        chain.link(nc.vector.reciprocal(inv_sum[:, :], inv_sum[:, :]))
                        nc.vector.tensor_tensor(upd[:, :], upd_ps[:, gs % 2, 0:GW], inv_sum[:, :], ALU.mult)\
                            .then_inc(upd_normed, 1)
                    if gs >= 0 and phase == 1:
                        wait(dve, nexp_ready, nth(i, GSTEPS, gs + 1))
                        chain.link(nc.vector.tensor_scalar(cand[:, :], nexp[:, :], 1.0, None, ALU.add))
                        chain.link(nc.vector.reciprocal(cand[:, :], cand[:, :]))
                        nc.vector.tensor_scalar(cand[:, :], cand[:, :], 2.0, -1.0, ALU.mult, ALU.add)\
                            .then_inc(cand_ready, 1)
                    if 1 <= n <= STEPS:
                        s = n - 1
                        wait(dve, exp_ready, nth(i, STEPS, s + 1))
                        nc.vector.tensor_reduce(den[0:TP, s % 2], attn[0:TP, s % 4], AX_X, ALU.add).then_inc(den_ready, 1)
                        wait(dve, den_ready, nth(i, STEPS, s + 1))
                        wait_reuse(dve, attn_ready, i, STEPS, s - 1)
                        nc.vector.reciprocal(rden[0:TP, s % 2], den[0:TP, s % 2]).then_inc(rden_ready, 1)
                    if gs >= 0 and phase == 1 and gs < GSTEPS - 2:
                        make_qk(i, gs + 2, gs % 2)
                wait(dve, h_turned, nth(i, 1, 1))
                wait(dve, out_stored, nth(i, DMA, DMA))
                nc.vector.tensor_tensor(acc[:].rearrange("p t d -> p (t d)"), gru_ps[0:ROWS, 0, 0:RT * D],
                                        x_in[:].rearrange("p t d -> p (t d)"), ALU.add).then_inc(x1_ready, 1)
                wait(dve, x1_ready, nth(i, 1, 1))
                layernorm(acc, nth(i, LN_PER, 2))
                first, second = router_weights(i)
                chain.link(nc.vector.tensor_tensor(mix[:], first[:], second[:], ALU.add))
                chain.link(nc.vector.tensor_tensor(mix[:], mix[:], rs_p[:], ALU.mult))
                for e in range(EXPERTS + 1):
                    if more and e < EXPERTS:
                        sum_squares(i + 1, e)
                    if e >= 1:
                        wait(dve, down_ready, nth(i, EXPERTS, e))
                        if e >= 2:
                            wait(dve, mixed, nth(i, EXPERTS, e - 1))
                        for t in range(RT):
                            ins = nc.vector.scalar_tensor_tensor(
                                out=acc[:, t, :], in0=score_ps[0:ROWS, 2 + (e - 1) % 2, t * D:(t + 1) * D],
                                scalar=mix[:, t, e - 1:e], in1=acc[:, t, :], op0=ALU.mult, op1=ALU.add)
                        ins.then_inc(mixed, 1)
                        if more:
                            copy_ctx(i + 1, e - 1)
                    if more and e == 3:
                        wait(dve, x_loaded, nth(i + 1, DMA, DMA))
                        layernorm(x_in, nth(i + 1, LN_PER, 1))

            with dve.Fori(0, NPAIR - 1) as i:
                body(i, True)
            body(NPAIR - 1, False)


_INS = ['x', 'ctx_1024', 'L0_xattn_Wq', 'L0_xattn_Wk', 'L0_xattn_Wv', 'L0_xattn_gru_wih', 'L0_xattn_gru_whh',
        'L0_xattn_gru_bih', 'L0_xattn_gru_bhh', 'L0_xattn_slot_norm_w', 'L0_xattn_input_norm_w',
        'L0_ffn_router_w', 'L0_ffn_w1', 'L0_ffn_w2']
_OUT = ((32, 56, 128), 'float32')


def kernel(**inputs):
    import numpy as _np
    import concourse.bacc as _bacc
    from concourse import mybir as _mybir
    from concourse.bass_utils import run_bass_kernel_spmd as _run

    nc = _bacc.Bacc("TRN2", target_bir_lowering=False, num_devices=1)
    arrays, args = {}, []
    for name in _INS:
        a = _np.ascontiguousarray(inputs[name])
        arrays[f"in_{name}_dram"] = a
        args.append(nc.dram_tensor(f"in_{name}_dram", a.shape, _mybir.dt.from_np(a.dtype), kind="ExternalInput").ap())
    dt = _mybir.dt.from_np(_np.dtype(_OUT[1]))
    args.append(nc.dram_tensor("out_0_dram", _OUT[0], dt, kind="ExternalOutput").ap())
    slot_attention_moe(nc, *args)
    r = _run(nc, [arrays], core_ids=[0])
    return r.results[0]["out_0_dram"]
```

```python
from contextlib import ExitStack

import numpy as np

import concourse.bass as bass
from concourse import mybir
from concourse.alu_op_type import AluOpType as ALU

ACT = mybir.ActivationFunctionType
F32, F16 = mybir.dt.float32, mybir.dt.float16
AX_X = mybir.AxisListType.X

BATCH, SLOTS, D = 32, 56, 128
TOKENS = 1500
TP = 125
CHUNKS = TOKENS // TP
HALF = CHUNKS // 2
HI, LO = 0, 1
ITERS = 3
PAIR = 8
NPAIR = BATCH // PAIR
GROUP = 2
NG = PAIR // GROUP
GW = GROUP * SLOTS
PW = PAIR * SLOTS
ROWS = 2 * SLOTS
RT = PW // ROWS
STEPS = ITERS * PAIR
GSTEPS = ITERS * NG
RAW = 3
BANK = 512
TILE_TURNS = 2 * BANK // D
CTILES = 2 * CHUNKS // TILE_TURNS
EXPERTS, HIDDEN = 8, 512
HC = HIDDEN // D
CH = EXPERTS * HC
DOWN_LAG = 3
HRING = 4
PADW = PW + D - ROWS
WTILES = EXPERTS
SCALE = float(D) ** -0.5
CTX_UP, QK_UP, ATTN_UP, W_UP = 64.0, 64.0, 2.0 ** 15, 64.0
EPS_RMS, EPS_ATTN, EPS_LN = 1e-6, 1e-6, 1e-5
DMA = 16
XDMA_ROWS = 112


def slot_attention_moe(nc, x, ctx, wq, wk, wv, wih, whh, bih, bhh, slot_w, input_w, router, w1, w2, out):
    with ExitStack() as stack:
        def sb(name, shape, dt=F32):
            return stack.enter_context(nc.sbuf_tensor(name, shape, dt))

        def psum(name, shape):
            return stack.enter_context(nc.psum_tensor(name, shape, F32))

        def sem(name):
            return stack.enter_context(nc.semaphore(name))

        ctx_raw = sb("ctx_raw", [128, RAW, CHUNKS, D])
        ctx_rows = sb("ctx_rows", [128, PAIR, 2, CHUNKS, D], F16)
        ctx_cols = sb("ctx_cols", [128, PAIR, 2, CHUNKS, D], F16)
        ssq = sb("ssq", [128, 2, CHUNKS])
        ctx_ms = sb("ctx_ms", [128, 2, CHUNKS])
        ctx_rstd = sb("ctx_rstd", [128, 2, CHUNKS])
        soft = sb("soft", [128, 4, CHUNKS, SLOTS])
        attn = sb("attn", [128, 3, 2, CHUNKS, SLOTS], F16)
        top = sb("top", [128, 2, CHUNKS])
        den = sb("den", [128, 2, CHUNKS])
        rden = sb("rden", [128, 2, CHUNKS])
        h = sb("h", [128, NG, GW])
        q_scaled = sb("q_scaled", [128, GW])
        qk32 = sb("qk32", [128, GW])
        qk = sb("qk", [128, NG, 2, GW], F16)
        h_sq = sb("h_sq", [128, GW])
        h_ms = sb("h_ms", [GW, 1])
        h_rstd = sb("h_rstd", [GW, 1])
        rstd_diag = sb("rstd_diag", [GW, GW])
        gh_n = sb("gh_n", [128, GW])
        z_gate = sb("z_gate", [128, GW])
        z_rest = sb("z_rest", [128, GW])
        zh = sb("zh", [128, GW])
        inv_sum = sb("inv_sum", [128, GW])
        upd = sb("upd", [128, GW])
        gates = sb("gates", [128, 2 * GW])
        npre = sb("npre", [128, GW])
        cand = sb("cand", [128, GW])
        x_in = sb("x_in", [ROWS, RT, D])
        acc = sb("acc", [ROWS, RT, D])
        normed = sb("normed", [ROWS, RT, D])
        stats = sb("stats", [ROWS, RT, 6])
        mv = sb("mv", [ROWS, RT, 2])
        row_var = sb("row_var", [ROWS, RT])
        row_rstd = sb("row_rstd", [ROWS, RT])
        ycols = sb("ycols", [128, PW])
        ycols16 = sb("ycols16", [128, 2, PW], F16)
        hid32 = sb("hid32", [128, 2, PW])
        hidden = sb("hidden", [128, HRING, 2, PADW], F16)
        w1_t = sb("w1_t", [128, 2, EXPERTS, HIDDEN], F16)
        w2_t = sb("w2_t", [128, 2, EXPERTS, HIDDEN], F16)
        router_raw = sb("router_raw", [EXPERTS, D])
        router_t = sb("router_t", [128, EXPERTS])
        early = soft[:, :, :, :].rearrange("p r c k -> p (r c k)")
        stage = early[:, 0:2 * HC * D].rearrange("p (s c d) -> p s c d", s=2, c=HC)
        gru_raw = early[:, 2 * HC * D:2 * HC * D + 6 * D].rearrange("p (g d) -> p g d", d=D)
        wih_t = early[:, 2 * HC * D + 6 * D:2 * HC * D + 9 * D]
        wq_sb = sb("wq_sb", [128, D])
        wk_sb = sb("wk_sb", [128, D])
        wv_sb = sb("wv_sb", [128, D])
        wx_t = sb("wx_t", [128, 3 * D])
        wh_t = sb("wh_t", [128, 3 * D])
        wqk = sb("wqk", [128, D])
        vec_raw = sb("vec_raw", [8, D])
        vec = sb("vec", [128, 8])
        key_scale = sb("key_scale", [128, 1])
        value_scale = sb("value_scale", [128, 1])
        half_rz = sb("half_rz", [128, 2])
        ident = sb("ident", [128, 128])
        ones = sb("ones", [128, 128])
        ident16 = sb("ident16", [128, 128], F16)
        ones16 = sb("ones16", [128, 128], F16)
        half_col = sb("half_col", [128, 1])
        h_eps = sb("h_eps", [GW, 1])
        half_bhn = sb("half_bhn", [128, 1])
        eps16 = sb("eps16", [1, 2, SLOTS], F16)
        ssq_eps = sb("ssq_eps", [128, CHUNKS])
        var_eps = sb("var_eps", [ROWS, RT])
        spare = sb("spare", [128, 1])
        mhalf = sb("mhalf", [128, CHUNKS])
        rank = sb("rank", [ROWS, RT, EXPERTS])
        rs_z = sb("rs_z", [ROWS, RT, EXPERTS])
        rs_e = sb("rs_e", [ROWS, RT, EXPERTS])
        rs_p = sb("rs_p", [ROWS, RT, EXPERTS])
        rs_k = sb("rs_k", [ROWS, RT, EXPERTS])
        rs_1 = sb("rs_1", [ROWS, RT, EXPERTS])
        rs_q = sb("rs_q", [ROWS, RT, EXPERTS])
        rs_m = sb("rs_m", [ROWS, RT])
        mix = sb("mix", [ROWS, RT, EXPERTS])

        score_ps = psum("score_ps", [128, 4, 512])
        upd_ps = psum("upd_ps", [128, 2, 512])
        gru_ps = psum("gru_ps", [128, 2, 512])
        Q_COLS, RSTD_COLS, SSQ_COL = slice(0, GW), slice(GW, 2 * GW), slice(2 * GW, 2 * GW + 1)

        consts_ready = sem("consts_ready")
        wq_loaded, wk_loaded, wv_loaded = sem("wq_loaded"), sem("wk_loaded"), sem("wv_loaded")
        vec_loaded, gruw_loaded, router_loaded = sem("vec_loaded"), sem("gruw_loaded"), sem("router_loaded")
        stage_loaded = [sem("stage_loaded0"), sem("stage_loaded1")]
        ctx_loaded = [sem(f"ctx_loaded{r}") for r in range(RAW)]
        x_loaded, out_stored = sem("x_loaded"), sem("out_stored")
        setup_mm, setup_copied = sem("setup_mm"), sem("setup_copied")
        wtile_turned, wtile_copied = sem("wtile_turned"), sem("wtile_copied")
        squared, ssq_ready, ctx_scaled = sem("squared"), sem("ssq_ready"), sem("ctx_scaled")
        rows_hi_ready, rows_ready, ctx_turned = sem("rows_hi_ready"), sem("rows_ready"), sem("ctx_turned")
        cols_by_dve, cols_by_act = sem("cols_by_dve"), sem("cols_by_act")
        scores_ready, max_ready, shift_ready = sem("scores_ready"), sem("max_ready"), sem("shift_ready")
        exp_ready, den_ready, rden_ready = sem("exp_ready"), sem("den_ready"), sem("rden_ready")
        den_scaled, inv_ready, r_ghn_ready = sem("den_scaled"), sem("inv_ready"), sem("r_ghn_ready")
        soft_ready, attn_hi_ready, attn_ready = sem("soft_ready"), sem("attn_hi_ready"), sem("attn_ready")
        upd_ready, upd_normed = sem("upd_ready"), sem("upd_normed")
        gates_mm, gates_tanh, npre_ready = sem("gates_mm"), sem("gates_tanh"), sem("npre_ready")
        cand_ready, h_ready = sem("cand_ready"), sem("h_ready")
        h_squared = sem("h_squared")
        h_ms_ready, h_rstd_ready = sem("h_ms_ready"), sem("h_rstd_ready")
        diag_ready, rstd_spread = sem("diag_ready"), sem("rstd_spread")
        q_mm, q_ready = sem("q_mm"), sem("q_ready")
        qk32_ready, qk_hi_ready, qk_ready = sem("qk32_ready"), sem("qk_hi_ready"), sem("qk_ready")
        ghn_mm, ghn_ready, z_ready = sem("ghn_mm"), sem("ghn_ready"), sem("z_ready")
        zh_ready, cand_scaled = sem("zh_ready"), sem("cand_scaled")
        h_turned, x1_ready, var_ready, rstd_ready = sem("h_turned"), sem("x1_ready"), sem("var_ready"), sem("rstd_ready")
        pads_ready = sem("pads_ready")
        y_hi_ready, y_split = sem("y_hi_ready"), sem("y_split")
        wtile_hi = sem("wtile_hi")
        normed_ready, normed_turned, cols_ready = sem("normed_ready"), sem("normed_turned"), sem("cols_ready")
        logits_ready, router_shift, router_exp = sem("logits_ready"), sem("router_shift"), sem("router_exp")
        up_ready, gelu_ready, hid_hi_ready = sem("up_ready"), sem("gelu_ready"), sem("hid_hi_ready")
        hid_ready, down_ready, mixed = sem("hid_ready"), sem("down_ready"), sem("mixed")
        dve_order, act_order, pool_order = sem("dve_order"), sem("act_order"), sem("pool_order")

        LN_PER = 2

        def nth(i, per, n):
            return i * per + n

        def wait(eng, semaphore, value):
            eng.wait_ge(semaphore, value)

        def wait_reuse(eng, semaphore, i, per, n):
            if n >= 1:
                eng.wait_ge(semaphore, nth(i, per, n))

        class Chain:
            def __init__(self, eng, semaphore):
                self.eng, self.semaphore, self.base, self.count = eng, semaphore, 0, 0

            def enter(self, base):
                self.base, self.count = base, 0

            def link(self, ins):
                self.count += 1
                ins.then_inc(self.semaphore, 1)
                self.eng.wait_ge(self.semaphore, self.base + self.count)

        PRODUCTS = ((HI, HI), (HI, LO), (LO, HI))
        LAG = 3
        PREP = PAIR + 2
        EARLY = 2

        def early_at(n):
            b, rest = divmod(n - STEPS, GROUP)
            return b if 0 <= b < EARLY and rest == 0 else None


        ROUNDS = STEPS + LAG + 1

        def gates_at(n):
            gs, rest = divmod(n - LAG - 1, GROUP)
            return gs if 0 <= gs < GSTEPS and rest == 0 else None

        def slots_at(n):
            return gates_at(n - 1)

        def queries_at(n):
            m, rest = divmod(n + 2, GROUP)
            return m if rest == 0 and m < GSTEPS else None

        def squares(b):
            return ctx_cols[0:TP, b].rearrange("p h c d -> p (h c d)").bitcast(F32)\
                .rearrange("p (c d) -> p c d", c=CHUNKS)

        def cols_tile(b, t):
            flat = ctx_cols[:, b].rearrange("p h c d -> p (h c d)").bitcast(F32)
            return flat[:, t * BANK:(t + 1) * BANK]

        def raw_uses(b):
            return len(range(b % RAW, PAIR, RAW))

        def batch_of(i, b):
            return i * PAIR + b

        block = stack.enter_context(nc.Block())

        @block.sync
        def _(sp):
            def load_ctx(j, b):
                r = b % RAW
                src = ctx[batch_of(j, b):batch_of(j, b) + 1] if isinstance(j, int) else ctx[bass.ds(batch_of(j, b), 1)]
                src = src.rearrange("o (p c) d -> p (o c) d", c=CHUNKS)
                if b >= RAW:
                    wait(sp, rows_ready, nth(j, PAIR, b - RAW + 1))
                elif not (isinstance(j, int) and j == 0):
                    wait(sp, rows_ready, nth(j, PAIR, b + RAW * (raw_uses(b) - 1) + 1 - PAIR))
                sp.dma_start(ctx_raw[0:XDMA_ROWS, r], src[0:XDMA_ROWS]).then_inc(ctx_loaded[r], DMA)
                sp.dma_start(ctx_raw[XDMA_ROWS:TP, r], src[XDMA_ROWS:TP]).then_inc(ctx_loaded[r], DMA)

            def load_ctx_next(i, b):
                load_ctx(i + 1, b)

            def rows_of(t, j):
                j8 = t[j * PAIR:(j + 1) * PAIR] if isinstance(j, int) else t[bass.ds(j * PAIR, PAIR)]
                return j8.rearrange("(t b) k d -> (b k) t d", b=2)

            sp.dma_start(wq_sb[:], wq).then_inc(wq_loaded, DMA)
            sp.dma_start(wk_sb[:], wk).then_inc(wk_loaded, DMA)
            sp.dma_start(vec_raw[0:3, :], bih.rearrange("(g d) -> g d", d=D)).then_inc(vec_loaded, DMA)
            sp.dma_start(vec_raw[3:6, :], bhh.rearrange("(g d) -> g d", d=D)).then_inc(vec_loaded, DMA)
            sp.dma_start(vec_raw[6:7, :], slot_w.rearrange("(g d) -> g d", d=D)).then_inc(vec_loaded, DMA)
            sp.dma_start(vec_raw[7:8, :], input_w.rearrange("(g d) -> g d", d=D)).then_inc(vec_loaded, DMA)
            sp.dma_start(x_in[:], rows_of(x, 0)).then_inc(x_loaded, DMA)
            load_ctx(0, 0)
            sp.dma_start(wv_sb[:], wv).then_inc(wv_loaded, DMA)
            sp.dma_start(gru_raw[:, 0:3, :], wih.rearrange("(g p) d -> p g d", p=128)).then_inc(gruw_loaded, DMA)
            sp.dma_start(gru_raw[:, 3:6, :], whh.rearrange("(g p) d -> p g d", p=128)).then_inc(gruw_loaded, DMA)
            sp.dma_start(router_raw[:], router).then_inc(router_loaded, DMA)
            load_ctx(0, 1)
            load_ctx(0, 2)

            def load_weights(t):
                if t >= 2:
                    sp.wait_ge(wtile_turned, t - 1)
                if t < WTILES:
                    src = w1[t].rearrange("(c p) d -> p c d", p=128)
                else:
                    src = w2[t - WTILES].rearrange("d (c p) -> d c p", p=128)
                sp.dma_start(stage[:, t % 2], src).then_inc(stage_loaded[t % 2], DMA)

            load_weights(0)
            load_weights(1)
            for b in range(2, PAIR):
                for t in (2 * b - 2, 2 * b - 1):
                    load_weights(t)
                if b >= RAW:
                    load_ctx(0, b)
            for t in (2 * PAIR - 2, 2 * PAIR - 1):
                load_weights(t)

            def body(i, more):
                if more:
                    for b in range(RAW):
                        load_ctx_next(i, b)
                    wait(sp, x1_ready, nth(i, 1, 1))
                    sp.dma_start(x_in[:], rows_of(x, i + 1)).then_inc(x_loaded, DMA)
                    for b in range(RAW, PAIR):
                        load_ctx_next(i, b)
                wait(sp, mixed, nth(i, EXPERTS, EXPERTS))
                sp.dma_start(rows_of(out, i), acc[:]).then_inc(out_stored, DMA)

            with sp.Fori(0, NPAIR - 1) as i:
                body(i, True)
            body(NPAIR - 1, False)
            sp.wait_ge(out_stored, DMA * (NPAIR + 1))

        @block.tensor
        def _(pe):
            def turn_ctx(j, b, t):
                n = CTILES * b + t
                if t == 0:
                    wait(pe, rows_ready, nth(j, PAIR, b + 1))
                if t == 2:
                    wait_reuse(pe, cols_by_dve, j, PAIR, b + 1)
                else:
                    wait_reuse(pe, cols_by_act, j, 2 * PAIR, 2 * (b - 1) + t + 1)
                bank = upd_ps[:, n % 2, :].bitcast(F16)
                for k in range(TILE_TURNS):
                    part, c = divmod(TILE_TURNS * t + k, CHUNKS)
                    mm = pe.transpose(bank[:, k * D:(k + 1) * D], ctx_rows[:, b, part, c, :], ident16[:, :])
                mm.then_inc(ctx_turned, 1)

            def turn_normed(n):
                wait(pe, normed_ready, n)
                for t in range(RT):
                    mm = pe.transpose(gru_ps[:, 1, t * ROWS:(t + 1) * ROWS], normed[:, t, :],
                                      ident[0:ROWS, 0:ROWS])
                mm.then_inc(normed_turned, 1)

            def queries(i, m):
                g = m % NG
                wait(pe, h_squared, nth(i, GSTEPS, m + 1))
                pe.matmul(gru_ps[0:GW, 1, SSQ_COL], h_sq[:, :], ones[:, 0:1], start=True, stop=True)
                pe.matmul(gru_ps[:, 1, Q_COLS], wqk[:, :], h[:, g, :], start=True, stop=True).then_inc(q_mm, 1)

            def spread_rstd(i, m):
                wait(pe, diag_ready, nth(i, GSTEPS, m + 1))
                wait(pe, q_ready, nth(i, GSTEPS, m + 1))
                pe.matmul(gru_ps[:, 1, RSTD_COLS], ones[0:GW, :], rstd_diag[:, :], start=True, stop=True)\
                    .then_inc(rstd_spread, 1)

            def scores(i, s):
                b, g = s % PAIR, (s // GROUP) % NG
                if s % GROUP == 0:
                    wait(pe, qk_ready, nth(i, GSTEPS, s // GROUP + 1))
                if s < PAIR:
                    wait(pe, cols_by_dve, nth(i, PAIR, b + 1))
                    wait(pe, cols_by_act, nth(i, 2 * PAIR, 2 * (b + 1)))
                wait_reuse(pe, shift_ready, i, STEPS, s - 1)
                for c in range(CHUNKS):
                    o = (c % HALF) * SLOTS
                    for n, (cp, qp) in enumerate(PRODUCTS):
                        mm = pe.matmul(score_ps[:, 2 * (s % 2) + c // HALF, o:o + SLOTS], ctx_cols[:, b, cp, c, :],
                                       qk[:, g, qp, (b % GROUP) * SLOTS:(b % GROUP + 1) * SLOTS],
                                       start=(n == 0), stop=(n == 2))
                mm.then_inc(scores_ready, 1)

            def update(i, s):
                b, gs = s % PAIR, s // GROUP
                wait(pe, attn_ready, nth(i, STEPS, s + 1))
                if s % GROUP == 0:
                    wait_reuse(pe, upd_normed, i, GSTEPS, gs - 1)
                o = (b % GROUP) * SLOTS
                for c in range(CHUNKS):
                    for n, (cp, ap) in enumerate(PRODUCTS):
                        pe.matmul(upd_ps[:, gs % 2, o:o + SLOTS], ctx_rows[0:TP, b, cp, c, :],
                                  attn[0:TP, s % 3, ap, c, :], start=(c == 0 and n == 0),
                                  stop=(c == CHUNKS - 1 and n == 2))
                for c in range(CHUNKS):
                    for ap in (HI, LO):
                        mm = pe.matmul(upd_ps[:, gs % 2, GW + o:GW + o + SLOTS], ones16[0:TP, :],
                                       attn[0:TP, s % 3, ap, c, :], start=(c == 0 and ap == HI), stop=False)
                for part in (HI, LO):
                    mm = pe.matmul(upd_ps[:, gs % 2, GW + o:GW + o + SLOTS], ones16[0:1, :], eps16[0:1, part, :],
                                   start=False, stop=(part == LO))
                mm.then_inc(upd_ready, 1)

            GATE_COLS = [slice(k * GW, (k + 1) * GW) for k in range(4)]

            def gates_of_slots(i, gs):
                wait_reuse(pe, npre_ready, i, GSTEPS, gs)
                for part in range(3):
                    cols = GATE_COLS[part if part < 2 else 3]
                    mm = pe.matmul(gru_ps[:, 0, cols], wh_t[:, part * D:(part + 1) * D], h[:, gs % NG, :],
                                   start=(part == 0), stop=(part == 2), skip_group_check=True)
                mm.then_inc(ghn_mm, 1)

            def gates_of_updates(i, gs):
                wait(pe, upd_normed, nth(i, GSTEPS, gs + 1))
                wait(pe, ghn_ready, nth(i, GSTEPS, gs + 1))
                for part in range(3):
                    mm = pe.matmul(gru_ps[:, 0, GATE_COLS[part]], wx_t[:, part * D:(part + 1) * D], upd[:, :],
                                   start=False, stop=True, skip_group_check=True)
                mm.then_inc(gates_mm, 1)

            def up(i, n):
                e, c = divmod(n, HC)
                wait_reuse(pe, gelu_ready, i, CH, n - 1)
                for k, (wp, yp) in enumerate(PRODUCTS):
                    mm = pe.matmul(score_ps[:, n % 2, 0:PW], w1_t[:, wp, e, c * D:(c + 1) * D], ycols16[:, yp, :],
                                   start=(k == 0), stop=(k == 2))
                mm.then_inc(up_ready, 1)

            def down(i, n):
                e, c = divmod(n, HC)
                wait(pe, hid_ready, nth(i, CH, n + 1))
                if c == 0:
                    wait_reuse(pe, mixed, i, EXPERTS, e - 1)
                for t in range(RT):
                    for k, (hp, wp) in enumerate(PRODUCTS):
                        mm = pe.matmul(score_ps[:, 2 + e % 2, t * D:(t + 1) * D],
                                       hidden[:, n % HRING, hp, t * ROWS:t * ROWS + D],
                                       w2_t[:, wp, e, c * D:(c + 1) * D], start=(c == 0 and t == 0 and k == 0),
                                       stop=(c == HC - 1 and k == 2), skip_group_check=True)
                mm.then_inc(down_ready, 1)

            pe.wait_ge(consts_ready, 1)
            pe.wait_ge(vec_loaded, 4 * DMA)
            pe.transpose(gru_ps[:, 0, 0:8], vec_raw[:, :], ident[0:8, 0:8]).then_inc(setup_mm, 1)
            pe.wait_ge(wq_loaded, DMA)
            pe.wait_ge(wk_loaded, DMA)
            pe.matmul(score_ps[:, 0, 0:D], wq_sb[:, :], wk_sb[:, :], start=True, stop=True).then_inc(setup_mm, 1)
            turn_normed(1)
            pe.wait_ge(gruw_loaded, 2 * DMA)
            for side in range(2):
                for g in range(3):
                    mm = pe.transpose(score_ps[:, 1 + side, g * D:(g + 1) * D], gru_raw[:, 3 * side + g, :], ident[:, :])
                mm.then_inc(setup_mm, 1)
            pe.wait_ge(router_loaded, DMA)
            pe.transpose(score_ps[:, 3, 0:EXPERTS], router_raw[:, :], ident[0:EXPERTS, 0:EXPERTS]).then_inc(setup_mm, 1)
            pe.wait_ge(wv_loaded, DMA)
            pe.wait_ge(setup_copied, 5)
            pe.matmul(score_ps[:, 0, 0:3 * D], wv_sb[:, :], wih_t[:, :], start=True, stop=True).then_inc(setup_mm, 1)
            pe.wait_ge(setup_copied, 6)
            for e in range(PREP):
                for t in (2 * e, 2 * e + 1):
                    if t < 2 * WTILES:
                        pe.wait_ge(stage_loaded[t % 2], DMA * (t // 2 + 1))
                        if t >= 4:
                            pe.wait_ge(wtile_copied, t - 3)
                        for c in range(HC):
                            mm = pe.transpose(score_ps[:, t % 4, c * D:(c + 1) * D], stage[:, t % 2, c, :], ident[:, :])
                        mm.then_inc(wtile_turned, 1)
                if e >= 2:
                    for t in range(CTILES):
                        turn_ctx(0, e - 2, t)

            def body(i, more):
                wait(pe, cols_ready, nth(i, LN_PER, 1))
                queries(i, 0)
                spread_rstd(i, 0)
                scores(i, 0)
                for n in range(ROUNDS):
                    gs, m = gates_at(n), queries_at(n)
                    if LAG <= n < STEPS + LAG:
                        update(i, n - LAG)
                    if m is not None:
                        queries(i, m)
                    if gs is not None:
                        gates_of_slots(i, gs)
                    if n + 1 < STEPS:
                        scores(i, n + 1)
                    if m is not None:
                        spread_rstd(i, m)
                    if gs is not None:
                        gates_of_updates(i, gs)
                wait(pe, h_ready, nth(i, GSTEPS, GSTEPS))
                for t in range(RT):
                    cols = h[:, :, :].rearrange("p g w -> p (g w)")[:, t * ROWS:(t + 1) * ROWS]
                    mm = pe.transpose(gru_ps[0:ROWS, 0, t * D:(t + 1) * D], cols, ident[:, :])
                mm.then_inc(h_turned, 1)
                turn_normed(nth(i, LN_PER, 2))
                wait(pe, cols_ready, nth(i, LN_PER, 2))
                for t in range(RT):
                    mm = pe.matmul(gru_ps[0:ROWS, 0, t * EXPERTS:(t + 1) * EXPERTS],
                                   ycols[:, t * ROWS:(t + 1) * ROWS], router_t[:, :], start=True, stop=True)
                mm.then_inc(logits_ready, 1)
                if not isinstance(i, int) or i == 0:
                    pe.wait_ge(wtile_copied, 2 * WTILES)
                wait(pe, y_split, nth(i, 1, 1))
                for n in range(CH + DOWN_LAG):
                    if n < CH:
                        up(i, n)
                    if n >= DOWN_LAG:
                        down(i, n - DOWN_LAG)
                    e, c = divmod(n, HC)
                    if more and e >= 1 and c >= 1 and n < CH:
                        turn_ctx(i + 1, e - 1, c - 1)
                    if more and n == 4 * HC + 3:
                        turn_normed(nth(i + 1, LN_PER, 1))
                if more:
                    for t in range(CTILES):
                        turn_ctx(i + 1, PAIR - 1, t)

            with pe.Fori(0, NPAIR - 1) as i:
                body(i, True)
            body(NPAIR - 1, False)

        EXP_TANH = "exp_and_others"

        @block.scalar
        def _(act):
            def square_ctx(j, b):
                wait(act, ctx_loaded[b % RAW], nth(j, 2 * DMA * raw_uses(b), 2 * DMA * (b // RAW + 1)))
                nc.scalar.activation(squares(b), ctx_raw[0:TP, b % RAW], ACT.Square, scale=1.0 / CTX_UP)\
                    .then_inc(squared, 1)

            def rows_hi(j, b):
                wait(act, ctx_scaled, nth(j, PAIR, b + 1))
                nc.scalar.copy(ctx_rows[0:TP, b, HI], ctx_raw[0:TP, b % RAW]).then_inc(rows_hi_ready, 1)

            def copy_turned(j, b, t):
                wait(act, ctx_turned, nth(j, CTILES * PAIR, CTILES * b + t + 1))
                nc.scalar.copy(cols_tile(b, t), upd_ps[:, (CTILES * b + t) % 2, :]).then_inc(cols_by_act, 1)

            def copy_cols(dst, n):
                wait(act, normed_turned, n)
                nc.scalar.copy(dst, gru_ps[:, 1, 0:PW]).then_inc(cols_ready, 1)

            def square_h(i, m):
                if m >= NG:
                    wait(act, h_ready, nth(i, GSTEPS, m - NG + 1))
                wait_reuse(act, q_mm, i, GSTEPS, m)
                nc.scalar.activation(h_sq[:, :], h[:, m % NG, :], ACT.Square).then_inc(h_squared, 1)

            def sum_of_squares(i, m):
                wait(act, q_mm, nth(i, GSTEPS, m + 1))
                nc.scalar.activation(h_ms[:, :], gru_ps[0:GW, 1, SSQ_COL], ACT.Identity, bias=h_eps[:, :], scale=1.0)\
                    .then_inc(h_ms_ready, 1)

            def scale_q(i, m):
                nc.scalar.activation(q_scaled[:, :], gru_ps[:, 1, Q_COLS], ACT.Copy, scale=key_scale[:, :])\
                    .then_inc(q_ready, 1)

            def qk_hi(i, m):
                wait(act, qk32_ready, nth(i, GSTEPS, m + 1))
                nc.scalar.copy(qk[:, m % NG, HI, :], qk32[:, :]).then_inc(qk_hi_ready, 1)

            act.preload_act_table_set(EXP_TANH)
            act.wait_ge(pads_ready, 1)
            hflat = h[:, :, :].rearrange("p g w -> p (g w)")
            square_ctx(0, 0)
            copy_cols(hflat, 1)
            for e in range(PREP):
                if 1 <= e < PAIR:
                    square_ctx(0, e)
                for t in (2 * e, 2 * e + 1):
                    if t < 2 * WTILES:
                        act.wait_ge(wtile_turned, t + 1)
                        w = w1_t if t < WTILES else w2_t
                        nc.scalar.mul(w[:, HI, t % WTILES, :], score_ps[:, t % 4, :], W_UP).then_inc(wtile_hi, 1)
                if 1 <= e <= PAIR:
                    rows_hi(0, e - 1)
                if e >= 2:
                    for t in (1, 2):
                        copy_turned(0, e - 2, t)

            def body(i, more):
                act.preload_act_table_set(EXP_TANH)
                wait(act, cols_ready, nth(i, LN_PER, 1))
                square_h(i, 0)
                sum_of_squares(i, 0)
                scale_q(i, 0)
                qk_hi(i, 0)
                for n in range(ROUNDS):
                    gs, done, m = gates_at(n), slots_at(n), queries_at(n)
                    if m is not None:
                        square_h(i, m)
                        sum_of_squares(i, m)
                    if done is not None:
                        wait(act, gates_mm, nth(i, GSTEPS, done + 1))
                        for part in range(2):
                            nc.scalar.activation(gates[:, part * GW:(part + 1) * GW],
                                                 gru_ps[:, 0, part * GW:(part + 1) * GW], ACT.Tanh,
                                                 bias=half_rz[:, part:part + 1], scale=0.5).then_inc(gates_tanh, 1)
                    if 2 <= n < STEPS + 2:
                        s = n - 2
                        wait(act, soft_ready, nth(i, STEPS, s + 1))
                        wait_reuse(act, upd_ready, i, STEPS, s - 2)
                        nc.scalar.copy(attn[0:TP, s % 3, HI], soft[0:TP, s % 4]).then_inc(attn_hi_ready, 1)
                    if m is not None:
                        scale_q(i, m)
                    if gs is not None:
                        wait(act, ghn_mm, nth(i, GSTEPS, gs + 1))
                        nc.scalar.activation(gh_n[:, :], gru_ps[:, 0, 3 * GW:4 * GW], ACT.Identity,
                                             bias=half_bhn[:, :], scale=0.5).then_inc(ghn_ready, 1)
                    if done is not None:
                        wait(act, gates_tanh, nth(i, 2 * GSTEPS, 2 * done + 2))
                        wait_reuse(act, h_ready, i, GSTEPS, done)
                        nc.scalar.activation(z_gate[:, :], gates[:, GW:2 * GW], ACT.Identity, bias=half_col[:, :],
                                             scale=0.5).then_inc(z_ready, 1)
                        nc.scalar.activation(z_rest[:, :], gates[:, GW:2 * GW], ACT.Identity, bias=half_col[:, :],
                                             scale=-0.5)
                        wait(act, npre_ready, nth(i, GSTEPS, done + 1))
                        nc.scalar.activation(cand[:, :], npre[:, :], ACT.Tanh, bias=vec[:, 2:3])\
                            .then_inc(cand_ready, 1)
                    if n < STEPS:
                        wait(act, shift_ready, nth(i, STEPS, n + 1))
                        nc.scalar.activation(soft[0:TP, n % 4], soft[0:TP, n % 4], ACT.Exp, scale=1.0 / QK_UP)\
                            .then_inc(exp_ready, 1)
                    if more and early_at(n + 1) is not None:
                        square_ctx(i + 1, early_at(n + 1))
                    if m is not None:
                        qk_hi(i, m)
                wait(act, normed_turned, nth(i, LN_PER, 2))
                nc.scalar.copy(ycols16[:, HI, :], gru_ps[:, 1, 0:PW]).then_inc(y_hi_ready, 1)
                copy_cols(ycols[:, :], nth(i, LN_PER, 2))
                wait(act, router_shift, nth(i, 1, 1))
                nc.scalar.activation(rs_e[:], rs_z[:], ACT.Exp).then_inc(router_exp, 1)
                act.preload_act_table(ACT.Gelu)
                for n in range(CH):
                    wait(act, up_ready, nth(i, CH, n + 1))
                    wait_reuse(act, hid_ready, i, CH, n - 1)
                    nc.scalar.activation(hid32[:, n % 2, :], score_ps[:, n % 2, 0:PW], ACT.Gelu, scale=1.0 / W_UP)\
                        .then_inc(gelu_ready, 1)
                    wait(act, gelu_ready, nth(i, CH, n + 1))
                    wait_reuse(act, down_ready, i, CH, n - HRING + 1)
                    nc.scalar.copy(hidden[:, n % HRING, HI, 0:PW], hid32[:, n % 2, :]).then_inc(hid_hi_ready, 1)
                    e, c = divmod(n, HC)
                    if more:
                        if c == 0 and EARLY <= e + 1 < PAIR:
                            square_ctx(i + 1, e + 1)
                        if c == 1:
                            rows_hi(i + 1, e)
                        if e >= 1 and c in (2, 3):
                            copy_turned(i + 1, e - 1, c - 1)
                        if n == 4 * HC + 3:
                            copy_cols(hflat, nth(i + 1, LN_PER, 1))
                if more:
                    for t in (1, 2):
                        copy_turned(i + 1, PAIR - 1, t)

            with act.Fori(0, NPAIR - 1) as i:
                body(i, True)
            body(NPAIR - 1, False)

        @block.gpsimd
        def _(pool):
            chain = Chain(pool, pool_order)
            CTX_LINKS, LN_LINKS = 2, 1
            PRO = 4 + CTX_LINKS * PAIR + LN_LINKS
            PER = CTX_LINKS * PAIR + 2 * LN_LINKS

            def scale_ctx(j, b):
                r = b % 2
                wait(pool, ssq_ready, nth(j, PAIR, b + 1))
                chain.link(nc.gpsimd.tensor_tensor(ctx_ms[0:TP, r], ssq[0:TP, r], ssq_eps[0:TP, :], ALU.add))
                chain.link(nc.gpsimd.tensor_tensor(ctx_rstd[0:TP, r], ctx_ms[0:TP, r], mhalf[0:TP, :], ALU.pow))
                rows = ctx_raw[0:TP, b % RAW]
                nc.gpsimd.tensor_tensor(rows, rows, ctx_rstd[0:TP, r].unsqueeze(2).to_broadcast([TP, CHUNKS, D]),
                                        ALU.mult).then_inc(ctx_scaled, 1)

            def rstd_rows(n):
                wait(pool, var_ready, n)
                chain.link(nc.gpsimd.tensor_tensor(row_var[:, :], mv[:, :, 1], var_eps[:, :], ALU.add))
                nc.gpsimd.tensor_tensor(row_rstd[:, :], row_var[:, :], mhalf[0:ROWS, 0:RT], ALU.pow).then_inc(rstd_ready, 1)

            def rstd_h(i, m):
                wait(pool, h_ms_ready, nth(i, GSTEPS, m + 1))
                nc.gpsimd.tensor_tensor(h_rstd[:, :], h_ms[:, :], mhalf[0:GW, 0:1], ALU.pow).then_inc(h_rstd_ready, 1)

            chain.link(nc.gpsimd.memset(ones[:, :], 1.0))
            chain.link(nc.gpsimd.affine_select(out=ident[:, :], in_=ones[:, :], compare_op=ALU.is_equal, fill=0.0,
                                               base=0, pattern=[[-1, 128]], channel_multiplier=1))
            nc.gpsimd.memset(half_col[:, :], 0.5)
            nc.gpsimd.memset(h_eps[:, :], D * EPS_RMS)
            eps_hi = float(np.float16(EPS_ATTN * ATTN_UP))
            nc.gpsimd.memset(eps16[:, HI, :], eps_hi)
            nc.gpsimd.memset(eps16[:, LO, :], EPS_ATTN * ATTN_UP - eps_hi)
            nc.gpsimd.memset(ssq_eps[:, :], D * EPS_RMS / CTX_UP ** 2)
            nc.gpsimd.memset(var_eps[:, :], EPS_LN)
            for e in range(EXPERTS):
                nc.gpsimd.memset(rank[:, :, e], float(EXPERTS - e))
            chain.link(nc.gpsimd.memset(mhalf[:, :], -0.5))
            chain.link(nc.gpsimd.tensor_copy(ident16[:, :], ident[:, :]))
            nc.gpsimd.tensor_copy(ones16[:, :], ones[:, :]).then_inc(consts_ready, 1)
            rstd_rows(1)
            for b in range(PAIR):
                scale_ctx(0, b)

            def body(i, more):
                chain.enter(PRO + i * PER)
                rstd_h(i, 0)
                for n in range(ROUNDS):
                    done = slots_at(n)
                    if queries_at(n) is not None:
                        rstd_h(i, queries_at(n))
                    if 2 <= n < STEPS + 2:
                        s = n - 2
                        wait(pool, attn_hi_ready, nth(i, STEPS, s + 1))
                        nc.gpsimd.tensor_tensor(attn[0:TP, s % 3, LO], soft[0:TP, s % 4], attn[0:TP, s % 3, HI],
                                                ALU.subtract).then_inc(attn_ready, 1)
                    if done is not None:
                        wait(pool, z_ready, nth(i, GSTEPS, done + 1))
                        nc.gpsimd.tensor_tensor(zh[:, :], z_gate[:, :], h[:, done % NG, :], ALU.mult)\
                            .then_inc(zh_ready, 1)
                    if 1 <= n <= STEPS:
                        s = n - 1
                        wait(pool, rden_ready, nth(i, STEPS, s + 1))
                        a = soft[0:TP, s % 4]
                        nc.gpsimd.tensor_tensor(a, a, rden[0:TP, s % 2].unsqueeze(2).to_broadcast([TP, CHUNKS, SLOTS]),
                                                ALU.mult).then_inc(soft_ready, 1)
                    if more and n == STEPS + 1:
                        scale_ctx(i + 1, 0)
                rstd_rows(nth(i, LN_PER, 2))
                if more:
                    for e in range(1, EXPERTS):
                        scale_ctx(i + 1, e)
                        if e == 3:
                            rstd_rows(nth(i + 1, LN_PER, 1))

            with pool.Fori(0, NPAIR - 1) as i:
                body(i, True)
            body(NPAIR - 1, False)

        @block.vector
        def _(dve):
            chain = Chain(dve, dve_order)
            LN_LINKS, ROUTER_LINKS = 1, 17
            PRO = 2 + LN_LINKS
            PER = 2 * LN_LINKS + ROUTER_LINKS

            def sum_squares(j, b):
                wait(dve, squared, nth(j, PAIR, b + 1))
                wait_reuse(dve, ctx_scaled, j, PAIR, b - 1)
                nc.vector.tensor_reduce(ssq[0:TP, b % 2], squares(b), AX_X, ALU.add).then_inc(ssq_ready, 1)

            def rows_lo(j, b):
                wait(dve, rows_hi_ready, nth(j, PAIR, b + 1))
                nc.vector.tensor_tensor(ctx_rows[0:TP, b, LO], ctx_raw[0:TP, b % RAW], ctx_rows[0:TP, b, HI],
                                        ALU.subtract).then_inc(rows_ready, 1)

            def copy_turned(j, b):
                wait(dve, ctx_turned, nth(j, CTILES * PAIR, CTILES * b + 1))
                nc.vector.tensor_copy(cols_tile(b, 0), upd_ps[:, (CTILES * b) % 2, :]).then_inc(cols_by_dve, 1)

            def layernorm(src, n):
                for t in range(RT):
                    ins = nc.vector.bn_stats(stats[:, t, :], src[:, t, :])
                chain.link(ins)
                nc.vector.memset(spare[:, :], 0.0)
                for t in range(RT):
                    ins = nc.vector.bn_aggr(mv[:, t, :], stats[:, t, :])
                ins.then_inc(var_ready, 1)
                wait(dve, rstd_ready, n)
                for t in range(RT):
                    ins = nc.vector.tensor_scalar(normed[:, t, :], src[:, t, :], mv[:, t, 0:1], row_rstd[:, t:t + 1],
                                                  ALU.subtract, ALU.mult)
                ins.then_inc(normed_ready, 1)

            def place_rstd(i, m):
                wait(dve, h_rstd_ready, nth(i, GSTEPS, m + 1))
                wait_reuse(dve, rstd_spread, i, GSTEPS, m)
                nc.vector.tensor_scalar(rstd_diag[:, :], ident[0:GW, 0:GW], h_rstd[:, :], None, ALU.mult)\
                    .then_inc(diag_ready, 1)

            def scale_qk(i, m):
                wait(dve, q_ready, nth(i, GSTEPS, m + 1))
                wait(dve, rstd_spread, nth(i, GSTEPS, m + 1))
                nc.vector.tensor_tensor(qk32[:, :], gru_ps[:, 1, RSTD_COLS], q_scaled[:, :], ALU.mult)\
                    .then_inc(qk32_ready, 1)

            def qk_lo(i, m):
                wait(dve, qk_hi_ready, nth(i, GSTEPS, m + 1))
                nc.vector.tensor_tensor(qk[:, m % NG, LO, :], qk32[:, :], qk[:, m % NG, HI, :], ALU.subtract)\
                    .then_inc(qk_ready, 1)

            nc.vector.memset(ctx_rows[96:128].rearrange("p b h c d -> p (b h c d)"), 0.0).then_inc(pads_ready, 1)
            nc.vector.memset(hidden[:, :, :, PW:PADW], 0.0)
            dve.sem_inc(out_stored, DMA)
            dve.wait_ge(setup_mm, 1)
            chain.link(nc.vector.tensor_copy(vec[:, :], gru_ps[:, 0, 0:8]))
            nc.vector.tensor_scalar(key_scale[:, :], vec[:, 7:8], SCALE * D * QK_UP / CTX_UP, None, ALU.mult)
            nc.vector.tensor_scalar(half_bhn[:, :], vec[:, 5:6], 0.5, None, ALU.mult)
            nc.vector.tensor_scalar(value_scale[:, :], vec[:, 7:8], D ** 0.5 / CTX_UP, None, ALU.mult)
            chain.link(nc.vector.tensor_tensor(half_rz[:, :], vec[:, 0:2], vec[:, 3:5], ALU.add))
            nc.vector.tensor_scalar(half_rz[:, :], half_rz[:, :], 0.5, None, ALU.mult).then_inc(setup_copied, 1)
            dve.wait_ge(setup_mm, 2)
            nc.vector.tensor_scalar(wqk[:, :], score_ps[:, 0, 0:D], vec[:, 6:7], None, ALU.mult).then_inc(setup_copied, 1)
            dve.wait_ge(x_loaded, DMA)
            layernorm(x_in, 1)
            dve.wait_ge(setup_mm, 3)
            nc.vector.tensor_copy(wih_t[:, :], score_ps[:, 1, 0:3 * D]).then_inc(setup_copied, 1)
            dve.wait_ge(setup_mm, 4)
            nc.vector.tensor_copy(wh_t[:, :], score_ps[:, 2, 0:3 * D]).then_inc(setup_copied, 1)
            dve.wait_ge(setup_mm, 5)
            nc.vector.tensor_copy(router_t[:, :], score_ps[:, 3, 0:EXPERTS]).then_inc(setup_copied, 1)
            dve.wait_ge(setup_mm, 6)
            nc.vector.tensor_scalar(wx_t[:, :], score_ps[:, 0, 0:3 * D], value_scale[:, :], None, ALU.mult)\
                .then_inc(setup_copied, 1)
            for e in range(PREP):
                if e < PAIR:
                    sum_squares(0, e)
                for t in (2 * e, 2 * e + 1):
                    if t < 2 * WTILES:
                        dve.wait_ge(wtile_hi, t + 1)
                        w = w1_t if t < WTILES else w2_t
                        nc.vector.scalar_tensor_tensor(out=w[:, LO, t % WTILES, :], in0=score_ps[:, t % 4, :], scalar=W_UP,
                                                       in1=w[:, HI, t % WTILES, :], op0=ALU.mult, op1=ALU.subtract)\
                            .then_inc(wtile_copied, 1)
                if 1 <= e <= PAIR:
                    rows_lo(0, e - 1)
                if e >= 2:
                    copy_turned(0, e - 2)

            def router_weights(i):
                def wide(a):
                    return a.unsqueeze(2).to_broadcast([ROWS, RT, EXPERTS])
                logits = gru_ps[0:ROWS, 0, 0:RT * EXPERTS].rearrange("p (t e) -> p t e", e=EXPERTS)
                wait(dve, logits_ready, nth(i, 1, 1))
                chain.link(nc.vector.tensor_reduce(rs_m[:], logits, AX_X, ALU.max))
                nc.vector.tensor_tensor(rs_z[:], logits, wide(rs_m[:]), ALU.subtract).then_inc(router_shift, 1)
                wait(dve, router_exp, nth(i, 1, 1))
                chain.link(nc.vector.tensor_reduce(rs_m[:], rs_e[:], AX_X, ALU.add))
                chain.link(nc.vector.reciprocal(rs_m[:], rs_m[:]))
                chain.link(nc.vector.tensor_tensor(rs_p[:], rs_e[:], wide(rs_m[:]), ALU.mult))

                def largest(src, dst):
                    chain.link(nc.vector.tensor_reduce(rs_m[:], src[:], AX_X, ALU.max))
                    chain.link(nc.vector.tensor_tensor(rs_k[:], src[:], wide(rs_m[:]), ALU.is_equal))
                    chain.link(nc.vector.tensor_tensor(rs_k[:], rs_k[:], rank[:], ALU.mult))
                    chain.link(nc.vector.tensor_reduce(rs_m[:], rs_k[:], AX_X, ALU.max))
                    chain.link(nc.vector.tensor_tensor(dst[:], rs_k[:], wide(rs_m[:]), ALU.is_equal))

                largest(rs_p, rs_1)
                chain.link(nc.vector.scalar_tensor_tensor(out=rs_q[:], in0=rs_1[:], scalar=-2.0, in1=rs_p[:],
                                                          op0=ALU.mult, op1=ALU.add))
                largest(rs_q, rs_z)
                return rs_1, rs_z

            def body(i, more):
                chain.enter(PRO + i * PER)
                place_rstd(i, 0)
                scale_qk(i, 0)
                qk_lo(i, 0)
                for n in range(ROUNDS):
                    gs, done, m, s = gates_at(n), slots_at(n), queries_at(n), n - 1
                    if n < STEPS:
                        banks = score_ps[0:TP, 2 * (n % 2):2 * (n % 2) + 2, 0:HALF * SLOTS]\
                            .rearrange("p h (c k) -> p h c k", k=SLOTS)
                        wait(dve, scores_ready, nth(i, STEPS, n + 1))
                        nc.vector.tensor_reduce(top[0:TP, n % 2], banks, AX_X, ALU.max).then_inc(max_ready, 1)
                    if queries_at(n - 1) is not None:
                        qk_lo(i, queries_at(n - 1))
                    if 0 <= s < STEPS:
                        wait(dve, exp_ready, nth(i, STEPS, s + 1))
                        nc.vector.tensor_reduce(den[0:TP, s % 2], soft[0:TP, s % 4], AX_X, ALU.add).then_inc(den_ready, 1)
                    if done is not None:
                        wait(dve, ghn_ready, nth(i, GSTEPS, done + 1))
                        wait(dve, gates_tanh, nth(i, 2 * GSTEPS, 2 * done + 2))
                        nc.vector.scalar_tensor_tensor(out=npre[:, :], in0=gates[:, 0:GW], scalar=1.0, in1=gh_n[:, :],
                                                       op0=ALU.add, op1=ALU.mult).then_inc(r_ghn_ready, 1)
                        wait(dve, r_ghn_ready, nth(i, GSTEPS, done + 1))
                        nc.vector.tensor_tensor(npre[:, :], gru_ps[:, 0, 2 * GW:3 * GW], npre[:, :], ALU.add)\
                            .then_inc(npre_ready, 1)
                    if n < STEPS:
                        wait(dve, max_ready, nth(i, STEPS, n + 1))
                        wait_reuse(dve, attn_ready, i, STEPS, n - 3)
                        tops = top[0:TP, n % 2].rearrange("p (h c) -> p h c", h=2).unsqueeze(3)\
                            .to_broadcast([TP, 2, HALF, SLOTS])
                        nc.vector.tensor_tensor(soft[0:TP, n % 4].rearrange("p (h c) k -> p h c k", h=2), banks,
                                                tops, ALU.subtract).then_inc(shift_ready, 1)
                    if 0 <= s < STEPS:
                        wait(dve, den_ready, nth(i, STEPS, s + 1))
                        nc.vector.tensor_scalar(den[0:TP, s % 2], den[0:TP, s % 2], 1.0 / ATTN_UP, None, ALU.mult)\
                            .then_inc(den_scaled, 1)
                    if done is not None:
                        wait(dve, cand_ready, nth(i, GSTEPS, done + 1))
                        nc.vector.tensor_tensor(z_rest[:, :], z_rest[:, :], cand[:, :], ALU.mult).then_inc(cand_scaled, 1)
                    if m is not None:
                        place_rstd(i, m)
                    if 0 <= s < STEPS:
                        wait(dve, den_scaled, nth(i, STEPS, s + 1))
                        wait_reuse(dve, soft_ready, i, STEPS, s - 1)
                        nc.vector.reciprocal(rden[0:TP, s % 2], den[0:TP, s % 2]).then_inc(rden_ready, 1)
                    if done is not None:
                        wait(dve, cand_scaled, nth(i, GSTEPS, done + 1))
                        wait(dve, zh_ready, nth(i, GSTEPS, done + 1))
                        nc.vector.tensor_tensor(h[:, done % NG, :], z_rest[:, :], zh[:, :], ALU.add).then_inc(h_ready, 1)
                    if gs is not None:
                        wait(dve, upd_ready, nth(i, STEPS, GROUP * (gs + 1)))
                        nc.vector.reciprocal(inv_sum[:, :], upd_ps[:, gs % 2, GW:2 * GW]).then_inc(inv_ready, 1)
                    if m is not None:
                        scale_qk(i, m)
                    if gs is not None:
                        wait(dve, inv_ready, nth(i, GSTEPS, gs + 1))
                        nc.vector.tensor_tensor(upd[:, :], upd_ps[:, gs % 2, 0:GW], inv_sum[:, :], ALU.mult)\
                            .then_inc(upd_normed, 1)
                    if more and early_at(n) is not None:
                        sum_squares(i + 1, early_at(n))
                wait(dve, h_turned, nth(i, 1, 1))
                wait(dve, out_stored, nth(i, DMA, DMA))
                nc.vector.tensor_tensor(acc[:].rearrange("p t d -> p (t d)"), gru_ps[0:ROWS, 0, 0:RT * D],
                                        x_in[:].rearrange("p t d -> p (t d)"), ALU.add).then_inc(x1_ready, 1)
                wait(dve, x1_ready, nth(i, 1, 1))
                layernorm(acc, nth(i, LN_PER, 2))
                wait(dve, cols_ready, nth(i, LN_PER, 2))
                nc.vector.tensor_tensor(ycols16[:, LO, :], ycols[:, :], ycols16[:, HI, :], ALU.subtract)\
                    .then_inc(y_split, 1)
                first, second = router_weights(i)
                chain.link(nc.vector.tensor_tensor(mix[:], first[:], second[:], ALU.add))
                chain.link(nc.vector.scalar_tensor_tensor(out=mix[:], in0=mix[:], scalar=1.0 / W_UP, in1=rs_p[:],
                                                          op0=ALU.mult, op1=ALU.mult))
                for n in range(CH + HC):
                    e, c = divmod(n, HC)
                    if n < CH:
                        wait(dve, hid_hi_ready, nth(i, CH, n + 1))
                        nc.vector.tensor_tensor(hidden[:, n % HRING, LO, 0:PW], hid32[:, n % 2, :],
                                                hidden[:, n % HRING, HI, 0:PW], ALU.subtract).then_inc(hid_ready, 1)
                    if e >= 1 and c == 2:
                        wait(dve, down_ready, nth(i, CH, HC * e))
                        if e >= 2:
                            wait(dve, mixed, nth(i, EXPERTS, e - 1))
                        for t in range(RT):
                            ins = nc.vector.scalar_tensor_tensor(
                                out=acc[:, t, :], in0=score_ps[0:ROWS, 2 + (e - 1) % 2, t * D:(t + 1) * D],
                                scalar=mix[:, t, e - 1:e], in1=acc[:, t, :], op0=ALU.mult, op1=ALU.add)
                        ins.then_inc(mixed, 1)
                    if more:
                        if EARLY <= e + 1 < PAIR and c == 1:
                            sum_squares(i + 1, e + 1)
                        if e < PAIR and c == 3:
                            rows_lo(i + 1, e)
                        if 1 <= e < PAIR and c == 1:
                            copy_turned(i + 1, e - 1)
                        if n == 3 * HC + 3:
                            wait(dve, x_loaded, nth(i + 1, DMA, DMA))
                            layernorm(x_in, nth(i + 1, LN_PER, 1))
                if more:
                    copy_turned(i + 1, PAIR - 1)

            with dve.Fori(0, NPAIR - 1) as i:
                body(i, True)
            body(NPAIR - 1, False)


_INS = ['x', 'ctx_1024', 'L0_xattn_Wq', 'L0_xattn_Wk', 'L0_xattn_Wv', 'L0_xattn_gru_wih', 'L0_xattn_gru_whh',
        'L0_xattn_gru_bih', 'L0_xattn_gru_bhh', 'L0_xattn_slot_norm_w', 'L0_xattn_input_norm_w',
        'L0_ffn_router_w', 'L0_ffn_w1', 'L0_ffn_w2']
_OUT = ((32, 56, 128), 'float32')


def kernel(**inputs):
    import numpy as _np
    import concourse.bacc as _bacc
    from concourse import mybir as _mybir
    from concourse.bass_utils import run_bass_kernel_spmd as _run

    nc = _bacc.Bacc("TRN2", target_bir_lowering=False, num_devices=1)
    arrays, args = {}, []
    for name in _INS:
        a = _np.ascontiguousarray(inputs[name])
        arrays[f"in_{name}_dram"] = a
        args.append(nc.dram_tensor(f"in_{name}_dram", a.shape, _mybir.dt.from_np(a.dtype), kind="ExternalInput").ap())
    dt = _mybir.dt.from_np(_np.dtype(_OUT[1]))
    args.append(nc.dram_tensor("out_0_dram", _OUT[0], dt, kind="ExternalOutput").ap())
    slot_attention_moe(nc, *args)
    r = _run(nc, [arrays], core_ids=[0])
    return r.results[0]["out_0_dram"]
```

```python
from contextlib import ExitStack

import numpy as np

import concourse.bass as bass
from concourse import mybir
from concourse.alu_op_type import AluOpType as ALU

ACT = mybir.ActivationFunctionType
F32, F16 = mybir.dt.float32, mybir.dt.float16
AX_X = mybir.AxisListType.X

BATCH, SLOTS, D = 32, 56, 128
TOKENS = 1500
TP = 125
CHUNKS = TOKENS // TP
HALF = CHUNKS // 2
HI, LO = 0, 1
ITERS = 3
PAIR = 8
NPAIR = BATCH // PAIR
GROUP = 2
NG = PAIR // GROUP
GW = GROUP * SLOTS
PW = PAIR * SLOTS
ROWS = 2 * SLOTS
RT = PW // ROWS
STEPS = ITERS * PAIR
GSTEPS = ITERS * NG
RAW = 3
BANK = 512
TILE_TURNS = 2 * BANK // D
CTILES = 2 * CHUNKS // TILE_TURNS
EXPERTS, HIDDEN = 8, 512
HC = HIDDEN // D
CH = EXPERTS * HC
DOWN_LAG = CTILES
GRING = 3
HRING = 4
PADW = PW + D - ROWS
WTILES = EXPERTS
SCALE = float(D) ** -0.5
CTX_UP, QK_UP, ATTN_UP, W_UP = 64.0, 64.0, 2.0 ** 15, 64.0
EPS_RMS, EPS_ATTN, EPS_LN = 1e-6, 1e-6, 1e-5
DMA = 16
XDMA_ROWS = 112


def slot_attention_moe(nc, x, ctx, wq, wk, wv, wih, whh, bih, bhh, slot_w, input_w, router, w1, w2, out):
    with ExitStack() as stack:
        def sb(name, shape, dt=F32):
            return stack.enter_context(nc.sbuf_tensor(name, shape, dt))

        def psum(name, shape):
            return stack.enter_context(nc.psum_tensor(name, shape, F32))

        def sem(name):
            return stack.enter_context(nc.semaphore(name))

        ctx_raw = sb("ctx_raw", [128, RAW, CHUNKS, D])
        ctx_rows = sb("ctx_rows", [128, PAIR, 2, CHUNKS, D], F16)
        ctx_cols = sb("ctx_cols", [128, PAIR, 2, CHUNKS, D], F16)
        ssq = sb("ssq", [128, 2, CHUNKS])
        ctx_ms = sb("ctx_ms", [128, 2, CHUNKS])
        ctx_rstd = sb("ctx_rstd", [128, 2, CHUNKS])
        soft = sb("soft", [128, 4, CHUNKS, SLOTS])
        attn = sb("attn", [128, 3, 2, CHUNKS, SLOTS], F16)
        top = sb("top", [128, 2, CHUNKS])
        den = sb("den", [128, 2, CHUNKS])
        rden = sb("rden", [128, 2, CHUNKS])
        h = sb("h", [128, NG, GW])
        q_scaled = sb("q_scaled", [128, GW])
        qk32 = sb("qk32", [128, GW])
        qk = sb("qk", [128, NG, 2, GW], F16)
        h_sq = sb("h_sq", [128, GW])
        h_ms = sb("h_ms", [GW, 1])
        h_rstd = sb("h_rstd", [GW, 1])
        rstd_diag = sb("rstd_diag", [GW, GW])
        gh_n = sb("gh_n", [128, GW])
        z_gate = sb("z_gate", [128, GW])
        z_rest = sb("z_rest", [128, GW])
        zh = sb("zh", [128, GW])
        inv_sum = sb("inv_sum", [128, GW])
        upd = sb("upd", [128, GW])
        gates = sb("gates", [128, 2 * GW])
        npre = sb("npre", [128, GW])
        cand = sb("cand", [128, GW])
        x_in = sb("x_in", [ROWS, RT, D])
        acc = sb("acc", [ROWS, RT, D])
        normed = sb("normed", [ROWS, RT, D])
        stats = sb("stats", [ROWS, RT, 6])
        mv = sb("mv", [ROWS, RT, 2])
        row_var = sb("row_var", [ROWS, RT])
        row_rstd = sb("row_rstd", [ROWS, RT])
        ycols = sb("ycols", [128, PW])
        ycols16 = sb("ycols16", [128, 2, PW], F16)
        hid32 = sb("hid32", [128, GRING, PW])
        hidden = sb("hidden", [128, HRING, 2, PADW], F16)
        w1_t = sb("w1_t", [128, 2, EXPERTS, HIDDEN], F16)
        w2_t = sb("w2_t", [128, 2, EXPERTS, HIDDEN], F16)
        router_raw = sb("router_raw", [EXPERTS, D])
        router_t = sb("router_t", [128, EXPERTS])
        early = soft[:, :, :, :].rearrange("p r c k -> p (r c k)")
        stage = early[:, 0:2 * HC * D].rearrange("p (s c d) -> p s c d", s=2, c=HC)
        gru_raw = early[:, 2 * HC * D:2 * HC * D + 6 * D].rearrange("p (g d) -> p g d", d=D)
        wih_t = early[:, 2 * HC * D + 6 * D:2 * HC * D + 9 * D]
        wq_sb = sb("wq_sb", [128, D])
        wk_sb = sb("wk_sb", [128, D])
        wv_sb = sb("wv_sb", [128, D])
        wx_t = sb("wx_t", [128, 3 * D])
        wh_t = sb("wh_t", [128, 3 * D])
        wqk = sb("wqk", [128, D])
        vec_raw = sb("vec_raw", [8, D])
        vec = sb("vec", [128, 8])
        key_scale = sb("key_scale", [128, 1])
        value_scale = sb("value_scale", [128, 1])
        half_rz = sb("half_rz", [128, 2])
        ident = sb("ident", [128, 128])
        ones = sb("ones", [128, 128])
        ident16 = sb("ident16", [128, 128], F16)
        ones16 = sb("ones16", [128, 128], F16)
        half_col = sb("half_col", [128, 1])
        h_eps = sb("h_eps", [GW, 1])
        half_bhn = sb("half_bhn", [128, 1])
        eps16 = sb("eps16", [1, 2, SLOTS], F16)
        ssq_eps = sb("ssq_eps", [128, CHUNKS])
        var_eps = sb("var_eps", [ROWS, RT])
        spare = sb("spare", [128, 1])
        mhalf = sb("mhalf", [128, CHUNKS])
        rank = sb("rank", [ROWS, RT, EXPERTS])
        rs_z = sb("rs_z", [ROWS, RT, EXPERTS])
        rs_e = sb("rs_e", [ROWS, RT, EXPERTS])
        rs_p = sb("rs_p", [ROWS, RT, EXPERTS])
        rs_k = sb("rs_k", [ROWS, RT, EXPERTS])
        rs_1 = sb("rs_1", [ROWS, RT, EXPERTS])
        rs_q = sb("rs_q", [ROWS, RT, EXPERTS])
        rs_m = sb("rs_m", [ROWS, RT])
        mix = sb("mix", [ROWS, RT, EXPERTS])

        score_ps = psum("score_ps", [128, 4, 512])
        upd_ps = psum("upd_ps", [128, 2, 512])
        gru_ps = psum("gru_ps", [128, 2, 512])
        Q_COLS, RSTD_COLS, SSQ_COL = slice(0, GW), slice(GW, 2 * GW), slice(2 * GW, 2 * GW + 1)

        consts_ready = sem("consts_ready")
        wq_loaded, wk_loaded, wv_loaded = sem("wq_loaded"), sem("wk_loaded"), sem("wv_loaded")
        vec_loaded, gruw_loaded, router_loaded = sem("vec_loaded"), sem("gruw_loaded"), sem("router_loaded")
        stage_loaded = [sem("stage_loaded0"), sem("stage_loaded1")]
        ctx_loaded = [sem(f"ctx_loaded{r}") for r in range(RAW)]
        x_loaded, out_stored = sem("x_loaded"), sem("out_stored")
        setup_mm, setup_copied = sem("setup_mm"), sem("setup_copied")
        wtile_turned, wtile_copied = sem("wtile_turned"), sem("wtile_copied")
        squared, ssq_ready, ctx_scaled = sem("squared"), sem("ssq_ready"), sem("ctx_scaled")
        rows_hi_ready, rows_ready, ctx_turned = sem("rows_hi_ready"), sem("rows_ready"), sem("ctx_turned")
        cols_by_dve, cols_by_act = sem("cols_by_dve"), sem("cols_by_act")
        scores_ready, max_ready, shift_ready = sem("scores_ready"), sem("max_ready"), sem("shift_ready")
        exp_ready, den_ready, rden_ready = sem("exp_ready"), sem("den_ready"), sem("rden_ready")
        den_scaled, inv_ready, r_ghn_ready = sem("den_scaled"), sem("inv_ready"), sem("r_ghn_ready")
        soft_ready, attn_hi_ready, attn_ready = sem("soft_ready"), sem("attn_hi_ready"), sem("attn_ready")
        upd_ready, upd_normed = sem("upd_ready"), sem("upd_normed")
        gates_mm, gates_tanh, npre_ready = sem("gates_mm"), sem("gates_tanh"), sem("npre_ready")
        cand_ready, h_ready = sem("cand_ready"), sem("h_ready")
        h_squared = sem("h_squared")
        h_ms_ready, h_rstd_ready = sem("h_ms_ready"), sem("h_rstd_ready")
        diag_ready, rstd_spread = sem("diag_ready"), sem("rstd_spread")
        q_mm, q_ready = sem("q_mm"), sem("q_ready")
        qk32_ready, qk_hi_ready, qk_ready = sem("qk32_ready"), sem("qk_hi_ready"), sem("qk_ready")
        ghn_mm, ghn_ready, z_ready = sem("ghn_mm"), sem("ghn_ready"), sem("z_ready")
        zh_ready, cand_scaled = sem("zh_ready"), sem("cand_scaled")
        h_turned, x1_ready, var_ready, rstd_ready = sem("h_turned"), sem("x1_ready"), sem("var_ready"), sem("rstd_ready")
        zeros_ready, pads_filled = sem("zeros_ready"), sem("pads_filled")
        y_hi_ready, y_split = sem("y_hi_ready"), sem("y_split")
        wtile_hi = sem("wtile_hi")
        normed_ready, normed_turned, cols_ready = sem("normed_ready"), sem("normed_turned"), sem("cols_ready")
        logits_ready, router_shift, router_exp = sem("logits_ready"), sem("router_shift"), sem("router_exp")
        up_ready, gelu_ready, hid_hi_ready = sem("up_ready"), sem("gelu_ready"), sem("hid_hi_ready")
        hid_ready, down_ready, mixed = sem("hid_ready"), sem("down_ready"), sem("mixed")
        dve_order, pool_order = sem("dve_order"), sem("pool_order")

        LN_PER = 2
        LNT_PER = LN_PER * RT
        assert NG == RT and GW == ROWS

        def ln_tile(t):
            return RT + t + 1

        def tile_done_at(n):
            t, rest = divmod(n - LAG - GROUP - 1, GROUP)
            t -= GSTEPS - NG
            return t if 0 <= t < RT and rest == 0 else None

        def nth(i, per, n):
            return i * per + n

        def wait(eng, semaphore, value):
            eng.wait_ge(semaphore, value)

        def wait_reuse(eng, semaphore, i, per, n):
            if n >= 1:
                eng.wait_ge(semaphore, nth(i, per, n))

        class Chain:
            def __init__(self, eng, semaphore):
                self.eng, self.semaphore, self.base, self.count = eng, semaphore, 0, 0

            def enter(self, base):
                self.base, self.count = base, 0

            def link(self, ins):
                self.count += 1
                ins.then_inc(self.semaphore, 1)
                self.eng.wait_ge(self.semaphore, self.base + self.count)

        PRODUCTS = ((HI, HI), (HI, LO), (LO, HI))
        LAG = 3
        PREP = PAIR + 3
        EARLY = 2

        QUERIES_AT, SPREAD_AT = 5 * HC + 1, 6 * HC + 3

        def early_at(n):
            b, rest = divmod(n - STEPS, GROUP)
            return b if 0 <= b < EARLY and rest == 0 else None


        ROUNDS = STEPS + LAG + 1

        def gates_at(n):
            gs, rest = divmod(n - LAG - 1, GROUP)
            return gs if 0 <= gs < GSTEPS and rest == 0 else None

        def slots_at(n):
            return gates_at(n - 1)

        def queries_at(n):
            m, rest = divmod(n + 2, GROUP)
            return m if rest == 0 and m < GSTEPS else None

        def squares(b):
            return ctx_cols[0:TP, b].rearrange("p h c d -> p (h c d)").bitcast(F32)\
                .rearrange("p (c d) -> p c d", c=CHUNKS)

        def cols_tile(b, t):
            flat = ctx_cols[:, b].rearrange("p h c d -> p (h c d)").bitcast(F32)
            return flat[:, t * BANK:(t + 1) * BANK]

        def raw_uses(b):
            return len(range(b % RAW, PAIR, RAW))

        def batch_of(i, b):
            return i * PAIR + b

        block = stack.enter_context(nc.Block())

        @block.sync
        def _(sp):
            def load_ctx(j, b):
                r = b % RAW
                src = ctx[batch_of(j, b):batch_of(j, b) + 1] if isinstance(j, int) else ctx[bass.ds(batch_of(j, b), 1)]
                src = src.rearrange("o (p c) d -> p (o c) d", c=CHUNKS)
                if b >= RAW:
                    wait(sp, rows_ready, nth(j, PAIR, b - RAW + 1))
                elif not (isinstance(j, int) and j == 0):
                    wait(sp, rows_ready, nth(j, PAIR, b + RAW * (raw_uses(b) - 1) + 1 - PAIR))
                sp.dma_start(ctx_raw[0:XDMA_ROWS, r], src[0:XDMA_ROWS]).then_inc(ctx_loaded[r], DMA)
                sp.dma_start(ctx_raw[XDMA_ROWS:TP, r], src[XDMA_ROWS:TP]).then_inc(ctx_loaded[r], DMA)

            def load_ctx_next(i, b):
                load_ctx(i + 1, b)

            def rows_of(t, j):
                j8 = t[j * PAIR:(j + 1) * PAIR] if isinstance(j, int) else t[bass.ds(j * PAIR, PAIR)]
                return j8.rearrange("(t b) k d -> (b k) t d", b=2)

            sp.dma_start(wq_sb[:], wq).then_inc(wq_loaded, DMA)
            sp.dma_start(wk_sb[:], wk).then_inc(wk_loaded, DMA)
            sp.dma_start(vec_raw[0:3, :], bih.rearrange("(g d) -> g d", d=D)).then_inc(vec_loaded, DMA)
            sp.dma_start(vec_raw[3:6, :], bhh.rearrange("(g d) -> g d", d=D)).then_inc(vec_loaded, DMA)
            sp.dma_start(vec_raw[6:7, :], slot_w.rearrange("(g d) -> g d", d=D)).then_inc(vec_loaded, DMA)
            sp.dma_start(vec_raw[7:8, :], input_w.rearrange("(g d) -> g d", d=D)).then_inc(vec_loaded, DMA)
            sp.dma_start(x_in[:], rows_of(x, 0)).then_inc(x_loaded, DMA)
            load_ctx(0, 0)
            sp.dma_start(wv_sb[:], wv).then_inc(wv_loaded, DMA)
            sp.dma_start(gru_raw[:, 0:3, :], wih.rearrange("(g p) d -> p g d", p=128)).then_inc(gruw_loaded, DMA)
            sp.dma_start(gru_raw[:, 3:6, :], whh.rearrange("(g p) d -> p g d", p=128)).then_inc(gruw_loaded, DMA)
            sp.dma_start(router_raw[:], router).then_inc(router_loaded, DMA)
            load_ctx(0, 1)
            load_ctx(0, 2)

            zeros = hidden[0:128 - TP, :, :, :].rearrange("p r h w -> p (r h w)")[:, 0:2 * CHUNKS * D]
            sp.wait_ge(zeros_ready, 1)
            for b in range(PAIR):
                sp.dma_start(ctx_rows[TP:128, b].rearrange("p h c d -> p (h c d)"), zeros).then_inc(pads_filled, DMA)

            def load_weights(t):
                if t >= 2:
                    sp.wait_ge(wtile_turned, t - 1)
                if t < WTILES:
                    src = w1[t].rearrange("(c p) d -> p c d", p=128)
                else:
                    src = w2[t - WTILES].rearrange("d (c p) -> d c p", p=128)
                sp.dma_start(stage[:, t % 2], src).then_inc(stage_loaded[t % 2], DMA)

            load_weights(0)
            load_weights(1)
            for b in range(2, PAIR):
                for t in (2 * b - 2, 2 * b - 1):
                    load_weights(t)
                if b >= RAW:
                    load_ctx(0, b)
            for t in (2 * PAIR - 2, 2 * PAIR - 1):
                load_weights(t)

            def body(i, more):
                if more:
                    for b in range(RAW):
                        load_ctx_next(i, b)
                    wait(sp, x1_ready, nth(i, RT, RT))
                    sp.dma_start(x_in[:], rows_of(x, i + 1)).then_inc(x_loaded, DMA)
                    for b in range(RAW, PAIR):
                        load_ctx_next(i, b)
                wait(sp, mixed, nth(i, EXPERTS, EXPERTS))
                sp.dma_start(rows_of(out, i), acc[:]).then_inc(out_stored, DMA)

            with sp.Fori(0, NPAIR - 1) as i:
                body(i, True)
            body(NPAIR - 1, False)
            sp.wait_ge(out_stored, DMA * (NPAIR + 1))

        @block.tensor
        def _(pe):
            def turn_ctx(j, b, t):
                n = CTILES * b + t
                if t == 0:
                    wait(pe, rows_ready, nth(j, PAIR, b + 1))
                if t == 2:
                    wait_reuse(pe, cols_by_dve, j, PAIR, b + 1)
                else:
                    wait_reuse(pe, cols_by_act, j, 2 * PAIR, 2 * (b - 1) + t + 1)
                bank = upd_ps[:, n % 2, :].bitcast(F16)
                for k in range(TILE_TURNS):
                    part, c = divmod(TILE_TURNS * t + k, CHUNKS)
                    mm = pe.transpose(bank[:, k * D:(k + 1) * D], ctx_rows[:, b, part, c, :], ident16[:, :])
                mm.then_inc(ctx_turned, 1)

            def turn_normed(n):
                wait(pe, normed_ready, n)
                for t in range(RT):
                    mm = pe.transpose(gru_ps[:, 1, t * ROWS:(t + 1) * ROWS], normed[:, t, :],
                                      ident[0:ROWS, 0:ROWS])
                mm.then_inc(normed_turned, RT)

            def turn_slots(i, t):
                wait(pe, h_ready, nth(i, GSTEPS, GSTEPS - NG + t + 1))
                wait_reuse(pe, x1_ready, i, RT, t)
                pe.transpose(gru_ps[0:ROWS, 1, t * D:(t + 1) * D], h[:, t, :], ident[:, :]).then_inc(h_turned, 1)

            def turn_ffn_input(i, t):
                if t == 0:
                    wait(pe, shift_ready, nth(i, STEPS, STEPS))
                wait(pe, normed_ready, nth(i, LNT_PER, ln_tile(t)))
                pe.transpose(score_ps[:, 3, t * ROWS:(t + 1) * ROWS], normed[:, t, :], ident[0:ROWS, 0:ROWS])\
                    .then_inc(normed_turned, 1)

            def queries(i, m):
                g = m % NG
                wait(pe, h_squared, nth(i, GSTEPS, m + 1))
                pe.matmul(gru_ps[0:GW, 1, SSQ_COL], h_sq[:, :], ones[:, 0:1], start=True, stop=True)
                pe.matmul(gru_ps[:, 1, Q_COLS], wqk[:, :], h[:, g, :], start=True, stop=True).then_inc(q_mm, 1)

            def spread_rstd(i, m):
                wait(pe, diag_ready, nth(i, GSTEPS, m + 1))
                wait(pe, q_ready, nth(i, GSTEPS, m + 1))
                pe.matmul(gru_ps[:, 1, RSTD_COLS], ones[0:GW, :], rstd_diag[:, :], start=True, stop=True)\
                    .then_inc(rstd_spread, 1)

            def scores(i, s):
                b, g = s % PAIR, (s // GROUP) % NG
                if s % GROUP == 0:
                    wait(pe, qk_ready, nth(i, GSTEPS, s // GROUP + 1))
                if s < PAIR:
                    wait(pe, cols_by_dve, nth(i, PAIR, b + 1))
                    wait(pe, cols_by_act, nth(i, 2 * PAIR, 2 * (b + 1)))
                wait_reuse(pe, shift_ready, i, STEPS, s - 1)
                for c in range(CHUNKS):
                    o = (c % HALF) * SLOTS
                    for n, (cp, qp) in enumerate(PRODUCTS):
                        mm = pe.matmul(score_ps[:, 2 * (s % 2) + c // HALF, o:o + SLOTS], ctx_cols[:, b, cp, c, :],
                                       qk[:, g, qp, (b % GROUP) * SLOTS:(b % GROUP + 1) * SLOTS],
                                       start=(n == 0), stop=(n == 2))
                mm.then_inc(scores_ready, 1)

            def update(i, s):
                b, gs = s % PAIR, s // GROUP
                wait(pe, attn_ready, nth(i, STEPS, s + 1))
                if s % GROUP == 0:
                    wait_reuse(pe, upd_normed, i, GSTEPS, gs - 1)
                o = (b % GROUP) * SLOTS
                for c in range(CHUNKS):
                    for n, (cp, ap) in enumerate(PRODUCTS):
                        pe.matmul(upd_ps[:, gs % 2, o:o + SLOTS], ctx_rows[0:TP, b, cp, c, :],
                                  attn[0:TP, s % 3, ap, c, :], start=(c == 0 and n == 0),
                                  stop=(c == CHUNKS - 1 and n == 2))
                for c in range(CHUNKS):
                    for ap in (HI, LO):
                        mm = pe.matmul(upd_ps[:, gs % 2, GW + o:GW + o + SLOTS], ones16[0:TP, :],
                                       attn[0:TP, s % 3, ap, c, :], start=(c == 0 and ap == HI), stop=False)
                for part in (HI, LO):
                    mm = pe.matmul(upd_ps[:, gs % 2, GW + o:GW + o + SLOTS], ones16[0:1, :], eps16[0:1, part, :],
                                   start=False, stop=(part == LO))
                mm.then_inc(upd_ready, 1)

            GATE_COLS = [slice(k * GW, (k + 1) * GW) for k in range(4)]

            def gates_of_slots(i, gs):
                wait_reuse(pe, npre_ready, i, GSTEPS, gs)
                for part in range(3):
                    cols = GATE_COLS[part if part < 2 else 3]
                    mm = pe.matmul(gru_ps[:, 0, cols], wh_t[:, part * D:(part + 1) * D], h[:, gs % NG, :],
                                   start=(part == 0), stop=(part == 2), skip_group_check=True)
                mm.then_inc(ghn_mm, 1)

            def gates_of_updates(i, gs):
                wait(pe, upd_normed, nth(i, GSTEPS, gs + 1))
                wait(pe, ghn_ready, nth(i, GSTEPS, gs + 1))
                for part in range(3):
                    mm = pe.matmul(gru_ps[:, 0, GATE_COLS[part]], wx_t[:, part * D:(part + 1) * D], upd[:, :],
                                   start=False, stop=True, skip_group_check=True)
                mm.then_inc(gates_mm, 1)

            def up(i, n):
                e, c = divmod(n, HC)
                wait_reuse(pe, gelu_ready, i, CH, n - 1)
                for k, (wp, yp) in enumerate(PRODUCTS):
                    mm = pe.matmul(score_ps[:, n % 2, 0:PW], w1_t[:, wp, e, c * D:(c + 1) * D], ycols16[:, yp, :],
                                   start=(k == 0), stop=(k == 2))
                mm.then_inc(up_ready, 1)

            def down(i, n):
                e, c = divmod(n, HC)
                wait(pe, hid_ready, nth(i, CH, n + 1))
                if c == 0:
                    wait_reuse(pe, mixed, i, EXPERTS, e - 1)
                for t in range(RT):
                    for k, (hp, wp) in enumerate(PRODUCTS):
                        mm = pe.matmul(score_ps[:, 2 + e % 2, t * D:(t + 1) * D],
                                       hidden[:, n % HRING, hp, t * ROWS:t * ROWS + D],
                                       w2_t[:, wp, e, c * D:(c + 1) * D], start=(c == 0 and t == 0 and k == 0),
                                       stop=(c == HC - 1 and k == 2), skip_group_check=True)
                mm.then_inc(down_ready, 1)

            pe.wait_ge(consts_ready, 1)
            pe.wait_ge(vec_loaded, 4 * DMA)
            pe.transpose(gru_ps[:, 0, 0:8], vec_raw[:, :], ident[0:8, 0:8]).then_inc(setup_mm, 1)
            pe.wait_ge(wq_loaded, DMA)
            pe.wait_ge(wk_loaded, DMA)
            pe.matmul(score_ps[:, 0, 0:D], wq_sb[:, :], wk_sb[:, :], start=True, stop=True).then_inc(setup_mm, 1)
            turn_normed(RT)
            pe.wait_ge(gruw_loaded, 2 * DMA)
            for side in range(2):
                for g in range(3):
                    mm = pe.transpose(score_ps[:, 1 + side, g * D:(g + 1) * D], gru_raw[:, 3 * side + g, :], ident[:, :])
                mm.then_inc(setup_mm, 1)
            pe.wait_ge(router_loaded, DMA)
            pe.transpose(score_ps[:, 3, 0:EXPERTS], router_raw[:, :], ident[0:EXPERTS, 0:EXPERTS]).then_inc(setup_mm, 1)
            pe.wait_ge(wv_loaded, DMA)
            pe.wait_ge(setup_copied, 5)
            pe.matmul(score_ps[:, 0, 0:3 * D], wv_sb[:, :], wih_t[:, :], start=True, stop=True).then_inc(setup_mm, 1)
            pe.wait_ge(setup_copied, 6)
            pe.wait_ge(pads_filled, DMA * PAIR)
            for e in range(PREP):
                if e >= 3:
                    for t in range(CTILES):
                        turn_ctx(0, e - 3, t)
                for t in (2 * e, 2 * e + 1):
                    if t < 2 * WTILES:
                        pe.wait_ge(stage_loaded[t % 2], DMA * (t // 2 + 1))
                        if t >= 4:
                            pe.wait_ge(wtile_copied, t - 3)
                        for c in range(HC):
                            mm = pe.transpose(score_ps[:, t % 4, c * D:(c + 1) * D], stage[:, t % 2, c, :], ident[:, :])
                        mm.then_inc(wtile_turned, 1)

            queries(0, 0)
            spread_rstd(0, 0)
            scores(0, 0)

            def body(i, more):
                for n in range(ROUNDS):
                    gs, m = gates_at(n), queries_at(n)
                    if gs is not None:
                        gates_of_slots(i, gs)
                    if m is not None:
                        queries(i, m)
                    if LAG <= n < STEPS + LAG:
                        update(i, n - LAG)
                    if m is not None:
                        spread_rstd(i, m)
                    if n + 1 < STEPS:
                        scores(i, n + 1)
                    if tile_done_at(n) is not None and tile_done_at(n) < RT - 1:
                        turn_slots(i, tile_done_at(n))
                    if gs is not None:
                        gates_of_updates(i, gs)
                    if n >= STEPS and tile_done_at(n) is not None:
                        turn_ffn_input(i, tile_done_at(n) - 1)
                turn_slots(i, RT - 1)
                turn_ffn_input(i, RT - 2)
                turn_ffn_input(i, RT - 1)
                wait(pe, cols_ready, nth(i, LN_PER, 2))
                for t in range(RT):
                    mm = pe.matmul(gru_ps[0:ROWS, 0, t * EXPERTS:(t + 1) * EXPERTS],
                                   ycols[:, t * ROWS:(t + 1) * ROWS], router_t[:, :], start=True, stop=True)
                mm.then_inc(logits_ready, 1)
                if not isinstance(i, int) or i == 0:
                    pe.wait_ge(wtile_copied, 2 * WTILES)
                wait(pe, y_split, nth(i, 1, 1))
                for n in range(CH + DOWN_LAG):
                    if n < CH:
                        up(i, n)
                    if n >= DOWN_LAG:
                        down(i, n - DOWN_LAG)
                    if more and n >= CH:
                        turn_ctx(i + 1, PAIR - 1, n - CH)
                    e, c = divmod(n, HC)
                    if more and e >= 1 and c >= 1 and n < CH:
                        turn_ctx(i + 1, e - 1, c - 1)
                    if more and n == 4 * HC + 3:
                        turn_normed(nth(i + 1, LNT_PER, RT))
                    if more and n == QUERIES_AT:
                        queries(i + 1, 0)
                    if more and n == SPREAD_AT:
                        spread_rstd(i + 1, 0)
                if more:
                    scores(i + 1, 0)
                    wait(pe, mixed, nth(i, EXPERTS, EXPERTS))

            with pe.Fori(0, NPAIR - 1) as i:
                body(i, True)
            body(NPAIR - 1, False)

        EXP_TANH = "exp_and_others"

        @block.scalar
        def _(act):
            def square_ctx(j, b):
                wait(act, ctx_loaded[b % RAW], nth(j, 2 * DMA * raw_uses(b), 2 * DMA * (b // RAW + 1)))
                nc.scalar.activation(squares(b), ctx_raw[0:TP, b % RAW], ACT.Square, scale=1.0 / CTX_UP)\
                    .then_inc(squared, 1)

            def rows_hi(j, b):
                wait(act, ctx_scaled, nth(j, PAIR, b + 1))
                nc.scalar.copy(ctx_rows[0:TP, b, HI], ctx_raw[0:TP, b % RAW]).then_inc(rows_hi_ready, 1)

            def copy_turned(j, b, t):
                wait(act, ctx_turned, nth(j, CTILES * PAIR, CTILES * b + t + 1))
                nc.scalar.copy(cols_tile(b, t), upd_ps[:, (CTILES * b + t) % 2, :]).then_inc(cols_by_act, 1)

            def copy_cols(dst, bank, n):
                wait(act, normed_turned, n)
                nc.scalar.copy(dst, bank[:, 0:PW]).then_inc(cols_ready, 1)

            def square_h(i, m):
                if m >= NG:
                    wait(act, h_ready, nth(i, GSTEPS, m - NG + 1))
                wait_reuse(act, q_mm, i, GSTEPS, m)
                nc.scalar.activation(h_sq[:, :], h[:, m % NG, :], ACT.Square).then_inc(h_squared, 1)

            def sum_of_squares(i, m):
                wait(act, q_mm, nth(i, GSTEPS, m + 1))
                nc.scalar.activation(h_ms[:, :], gru_ps[0:GW, 1, SSQ_COL], ACT.Identity, bias=h_eps[:, :], scale=1.0)\
                    .then_inc(h_ms_ready, 1)

            def scale_q(i, m):
                nc.scalar.activation(q_scaled[:, :], gru_ps[:, 1, Q_COLS], ACT.Copy, scale=key_scale[:, :])\
                    .then_inc(q_ready, 1)

            def qk_hi(i, m):
                wait(act, qk32_ready, nth(i, GSTEPS, m + 1))
                nc.scalar.copy(qk[:, m % NG, HI, :], qk32[:, :]).then_inc(qk_hi_ready, 1)

            act.preload_act_table_set(EXP_TANH)
            hflat = h[:, :, :].rearrange("p g w -> p (g w)")
            square_ctx(0, 0)
            copy_cols(hflat, gru_ps[:, 1], RT)
            for e in range(PREP):
                if 1 <= e < PAIR:
                    square_ctx(0, e)
                if e >= 3:
                    for t in (1, 2):
                        copy_turned(0, e - 3, t)
                for t in (2 * e, 2 * e + 1):
                    if t < 2 * WTILES:
                        act.wait_ge(wtile_turned, t + 1)
                        w = w1_t if t < WTILES else w2_t
                        nc.scalar.mul(w[:, HI, t % WTILES, :], score_ps[:, t % 4, :], W_UP).then_inc(wtile_hi, 1)
                if 1 <= e <= PAIR:
                    rows_hi(0, e - 1)

            square_h(0, 0)
            sum_of_squares(0, 0)
            scale_q(0, 0)
            qk_hi(0, 0)

            def body(i, more):
                for n in range(ROUNDS):
                    gs, done, m = gates_at(n), slots_at(n), queries_at(n)
                    if m is not None:
                        square_h(i, m)
                        sum_of_squares(i, m)
                    if done is not None:
                        wait(act, gates_mm, nth(i, GSTEPS, done + 1))
                        for part in range(2):
                            nc.scalar.activation(gates[:, part * GW:(part + 1) * GW],
                                                 gru_ps[:, 0, part * GW:(part + 1) * GW], ACT.Tanh,
                                                 bias=half_rz[:, part:part + 1], scale=0.5).then_inc(gates_tanh, 1)
                        wait(act, gates_tanh, nth(i, 2 * GSTEPS, 2 * done + 2))
                        wait_reuse(act, h_ready, i, GSTEPS, done)
                        nc.scalar.activation(z_gate[:, :], gates[:, GW:2 * GW], ACT.Identity, bias=half_col[:, :],
                                             scale=0.5).then_inc(z_ready, 1)
                    if 2 <= n < STEPS + 2:
                        s = n - 2
                        wait(act, soft_ready, nth(i, STEPS, s + 1))
                        wait_reuse(act, upd_ready, i, STEPS, s - 2)
                        nc.scalar.copy(attn[0:TP, s % 3, HI], soft[0:TP, s % 4]).then_inc(attn_hi_ready, 1)
                    if m is not None:
                        scale_q(i, m)
                    if gs is not None:
                        wait(act, ghn_mm, nth(i, GSTEPS, gs + 1))
                        nc.scalar.activation(gh_n[:, :], gru_ps[:, 0, 3 * GW:4 * GW], ACT.Identity,
                                             bias=half_bhn[:, :], scale=0.5).then_inc(ghn_ready, 1)
                    if done is not None:
                        nc.scalar.activation(z_rest[:, :], gates[:, GW:2 * GW], ACT.Identity, bias=half_col[:, :],
                                             scale=-0.5)
                        wait(act, npre_ready, nth(i, GSTEPS, done + 1))
                        nc.scalar.activation(cand[:, :], npre[:, :], ACT.Tanh, bias=vec[:, 2:3])\
                            .then_inc(cand_ready, 1)
                    if n < STEPS:
                        wait(act, shift_ready, nth(i, STEPS, n + 1))
                        nc.scalar.activation(soft[0:TP, n % 4], soft[0:TP, n % 4], ACT.Exp, scale=1.0 / QK_UP)\
                            .then_inc(exp_ready, 1)
                    if more and early_at(n + 1) is not None:
                        square_ctx(i + 1, early_at(n + 1))
                    if m is not None:
                        qk_hi(i, m)
                copy_cols(ycols[:, :], score_ps[:, 3], nth(i, LNT_PER, ln_tile(RT - 1)))
                nc.scalar.copy(ycols16[:, HI, :], score_ps[:, 3, 0:PW]).then_inc(y_hi_ready, 1)
                wait(act, router_shift, nth(i, 1, 1))
                nc.scalar.activation(rs_e[:], rs_z[:], ACT.Exp).then_inc(router_exp, 1)
                act.preload_act_table(ACT.Gelu)
                def hid_hi(n):
                    wait(act, gelu_ready, nth(i, CH, n + 1))
                    wait_reuse(act, down_ready, i, CH, n - HRING + 1)
                    nc.scalar.copy(hidden[:, n % HRING, HI, 0:PW], hid32[:, n % GRING, :]).then_inc(hid_hi_ready, 1)

                for n in range(CH):
                    wait(act, up_ready, nth(i, CH, n + 1))
                    wait_reuse(act, hid_ready, i, CH, n - GRING + 1)
                    nc.scalar.activation(hid32[:, n % GRING, :], score_ps[:, n % 2, 0:PW], ACT.Gelu,
                                         scale=1.0 / W_UP).then_inc(gelu_ready, 1)
                    if n >= 1:
                        hid_hi(n - 1)
                    e, c = divmod(n, HC)
                    if more:
                        if c == 0 and EARLY <= e + 1 < PAIR:
                            square_ctx(i + 1, e + 1)
                        if c == 1:
                            rows_hi(i + 1, e)
                        if e >= 1 and c in (2, 3):
                            copy_turned(i + 1, e - 1, c - 1)
                        if n == 4 * HC + 3:
                            copy_cols(hflat, gru_ps[:, 1], nth(i + 1, LNT_PER, RT))
                        if n == QUERIES_AT - 1:
                            wait(act, cols_ready, nth(i + 1, LN_PER, 1))
                            square_h(i + 1, 0)
                        if n == QUERIES_AT + 1:
                            sum_of_squares(i + 1, 0)
                            scale_q(i + 1, 0)
                        if n == SPREAD_AT + 2:
                            qk_hi(i + 1, 0)
                if more:
                    act.preload_act_table_set(EXP_TANH)
                hid_hi(CH - 1)
                if more:
                    for t in (1, 2):
                        copy_turned(i + 1, PAIR - 1, t)

            with act.Fori(0, NPAIR - 1) as i:
                body(i, True)
            body(NPAIR - 1, False)

        @block.gpsimd
        def _(pool):
            chain = Chain(pool, pool_order)
            CTX_LINKS, LN_LINKS = 2, 1
            PRO = 4 + CTX_LINKS * PAIR + LN_LINKS
            PER = CTX_LINKS * PAIR + LN_LINKS + LN_LINKS * RT

            def scale_ctx(j, b):
                r = b % 2
                wait(pool, ssq_ready, nth(j, PAIR, b + 1))
                chain.link(nc.gpsimd.tensor_tensor(ctx_ms[0:TP, r], ssq[0:TP, r], ssq_eps[0:TP, :], ALU.add))
                chain.link(nc.gpsimd.tensor_tensor(ctx_rstd[0:TP, r], ctx_ms[0:TP, r], mhalf[0:TP, :], ALU.pow))
                rows = ctx_raw[0:TP, b % RAW]
                nc.gpsimd.tensor_tensor(rows, rows, ctx_rstd[0:TP, r].unsqueeze(2).to_broadcast([TP, CHUNKS, D]),
                                        ALU.mult).then_inc(ctx_scaled, 1)

            def rstd_rows(n):
                wait(pool, var_ready, n)
                chain.link(nc.gpsimd.tensor_tensor(row_var[:, :], mv[:, :, 1], var_eps[:, :], ALU.add))
                nc.gpsimd.tensor_tensor(row_rstd[:, :], row_var[:, :], mhalf[0:ROWS, 0:RT], ALU.pow)\
                    .then_inc(rstd_ready, RT)

            def rstd_tile(i, t):
                wait(pool, var_ready, nth(i, LNT_PER, ln_tile(t)))
                chain.link(nc.gpsimd.tensor_tensor(row_var[:, t:t + 1], mv[:, t, 1:2], var_eps[:, 0:1], ALU.add))
                nc.gpsimd.tensor_tensor(row_rstd[:, t:t + 1], row_var[:, t:t + 1], mhalf[0:ROWS, 0:1], ALU.pow)\
                    .then_inc(rstd_ready, 1)

            def rstd_h(i, m):
                wait(pool, h_ms_ready, nth(i, GSTEPS, m + 1))
                nc.gpsimd.tensor_tensor(h_rstd[:, :], h_ms[:, :], mhalf[0:GW, 0:1], ALU.pow).then_inc(h_rstd_ready, 1)

            chain.link(nc.gpsimd.memset(ones[:, :], 1.0))
            chain.link(nc.gpsimd.affine_select(out=ident[:, :], in_=ones[:, :], compare_op=ALU.is_equal, fill=0.0,
                                               base=0, pattern=[[-1, 128]], channel_multiplier=1))
            nc.gpsimd.memset(half_col[:, :], 0.5)
            nc.gpsimd.memset(h_eps[:, :], D * EPS_RMS)
            eps_hi = float(np.float16(EPS_ATTN * ATTN_UP))
            nc.gpsimd.memset(eps16[:, HI, :], eps_hi)
            nc.gpsimd.memset(eps16[:, LO, :], EPS_ATTN * ATTN_UP - eps_hi)
            nc.gpsimd.memset(ssq_eps[:, :], D * EPS_RMS / CTX_UP ** 2)
            nc.gpsimd.memset(var_eps[:, :], EPS_LN)
            for e in range(EXPERTS):
                nc.gpsimd.memset(rank[:, :, e], float(EXPERTS - e))
            chain.link(nc.gpsimd.memset(mhalf[:, :], -0.5))
            chain.link(nc.gpsimd.tensor_copy(ident16[:, :], ident[:, :]))
            nc.gpsimd.tensor_copy(ones16[:, :], ones[:, :]).then_inc(consts_ready, 1)
            nc.gpsimd.memset(hidden[:, :, :, :].rearrange("p r h w -> p (r h w)"), 0.0).then_inc(zeros_ready, 1)
            rstd_rows(RT)
            for b in range(PAIR):
                scale_ctx(0, b)

            rstd_h(0, 0)

            def body(i, more):
                chain.enter(PRO + i * PER)
                for n in range(ROUNDS):
                    done = slots_at(n)
                    if queries_at(n) is not None:
                        rstd_h(i, queries_at(n))
                    if done is not None:
                        wait(pool, z_ready, nth(i, GSTEPS, done + 1))
                        nc.gpsimd.tensor_tensor(zh[:, :], z_gate[:, :], h[:, done % NG, :], ALU.mult)\
                            .then_inc(zh_ready, 1)
                    if 2 <= n < STEPS + 2:
                        s = n - 2
                        wait(pool, attn_hi_ready, nth(i, STEPS, s + 1))
                        nc.gpsimd.tensor_tensor(attn[0:TP, s % 3, LO], soft[0:TP, s % 4], attn[0:TP, s % 3, HI],
                                                ALU.subtract).then_inc(attn_ready, 1)
                    if 1 <= n <= STEPS:
                        s = n - 1
                        wait(pool, rden_ready, nth(i, STEPS, s + 1))
                        a = soft[0:TP, s % 4]
                        nc.gpsimd.tensor_tensor(a, a, rden[0:TP, s % 2].unsqueeze(2).to_broadcast([TP, CHUNKS, SLOTS]),
                                                ALU.mult).then_inc(soft_ready, 1)
                    if done is not None and tile_done_at(n - 1) is not None:
                        rstd_tile(i, tile_done_at(n - 1))
                    if more and n == STEPS + 1:
                        scale_ctx(i + 1, 0)
                rstd_tile(i, RT - 1)
                if more:
                    for e in range(1, EXPERTS):
                        scale_ctx(i + 1, e)
                        if e == EXPERTS - 2:
                            rstd_h(i + 1, 0)
                        if e == 3:
                            rstd_rows(nth(i + 1, LNT_PER, RT))

            with pool.Fori(0, NPAIR - 1) as i:
                body(i, True)
            body(NPAIR - 1, False)

        @block.vector
        def _(dve):
            chain = Chain(dve, dve_order)
            LN_LINKS, ROUTER_LINKS = 1, 17
            PRO = 2 + LN_LINKS
            PER = LN_LINKS + LN_LINKS * RT + ROUTER_LINKS

            def sum_squares(j, b):
                wait(dve, squared, nth(j, PAIR, b + 1))
                wait_reuse(dve, ctx_scaled, j, PAIR, b - 1)
                nc.vector.tensor_reduce(ssq[0:TP, b % 2], squares(b), AX_X, ALU.add).then_inc(ssq_ready, 1)

            def rows_lo(j, b):
                wait(dve, rows_hi_ready, nth(j, PAIR, b + 1))
                nc.vector.tensor_tensor(ctx_rows[0:TP, b, LO], ctx_raw[0:TP, b % RAW], ctx_rows[0:TP, b, HI],
                                        ALU.subtract).then_inc(rows_ready, 1)

            def copy_turned(j, b):
                wait(dve, ctx_turned, nth(j, CTILES * PAIR, CTILES * b + 1))
                nc.vector.tensor_copy(cols_tile(b, 0), upd_ps[:, (CTILES * b) % 2, :]).then_inc(cols_by_dve, 1)

            def layernorm(src, n):
                for t in range(RT):
                    ins = nc.vector.bn_stats(stats[:, t, :], src[:, t, :])
                chain.link(ins)
                nc.vector.memset(spare[:, :], 0.0)
                for t in range(RT):
                    ins = nc.vector.bn_aggr(mv[:, t, :], stats[:, t, :])
                ins.then_inc(var_ready, RT)
                wait(dve, rstd_ready, n)
                for t in range(RT):
                    ins = nc.vector.tensor_scalar(normed[:, t, :], src[:, t, :], mv[:, t, 0:1], row_rstd[:, t:t + 1],
                                                  ALU.subtract, ALU.mult)
                ins.then_inc(normed_ready, RT)

            def add_slots(i, t):
                wait(dve, h_turned, nth(i, RT, t + 1))
                if t == 0:
                    wait(dve, out_stored, nth(i, DMA, DMA))
                nc.vector.tensor_tensor(acc[:, t, :], gru_ps[0:ROWS, 1, t * D:(t + 1) * D], x_in[:, t, :], ALU.add)\
                    .then_inc(x1_ready, 1)
                wait(dve, x1_ready, nth(i, RT, t + 1))
                chain.link(nc.vector.bn_stats(stats[:, t, :], acc[:, t, :]))
                nc.vector.memset(spare[:, :], 0.0)
                nc.vector.bn_aggr(mv[:, t, :], stats[:, t, :]).then_inc(var_ready, 1)

            def norm_tile(i, t):
                wait(dve, rstd_ready, nth(i, LNT_PER, ln_tile(t)))
                nc.vector.tensor_scalar(normed[:, t, :], acc[:, t, :], mv[:, t, 0:1], row_rstd[:, t:t + 1],
                                        ALU.subtract, ALU.mult).then_inc(normed_ready, 1)

            def place_rstd(i, m):
                wait(dve, h_rstd_ready, nth(i, GSTEPS, m + 1))
                wait_reuse(dve, rstd_spread, i, GSTEPS, m)
                nc.vector.tensor_scalar(rstd_diag[:, :], ident[0:GW, 0:GW], h_rstd[:, :], None, ALU.mult)\
                    .then_inc(diag_ready, 1)

            def scale_qk(i, m):
                wait(dve, q_ready, nth(i, GSTEPS, m + 1))
                wait(dve, rstd_spread, nth(i, GSTEPS, m + 1))
                nc.vector.tensor_tensor(qk32[:, :], gru_ps[:, 1, RSTD_COLS], q_scaled[:, :], ALU.mult)\
                    .then_inc(qk32_ready, 1)

            def qk_lo(i, m):
                wait(dve, qk_hi_ready, nth(i, GSTEPS, m + 1))
                nc.vector.tensor_tensor(qk[:, m % NG, LO, :], qk32[:, :], qk[:, m % NG, HI, :], ALU.subtract)\
                    .then_inc(qk_ready, 1)

            dve.sem_inc(out_stored, DMA)
            dve.wait_ge(setup_mm, 1)
            chain.link(nc.vector.tensor_copy(vec[:, :], gru_ps[:, 0, 0:8]))
            nc.vector.tensor_scalar(key_scale[:, :], vec[:, 7:8], SCALE * D * QK_UP / CTX_UP, None, ALU.mult)
            nc.vector.tensor_scalar(half_bhn[:, :], vec[:, 5:6], 0.5, None, ALU.mult)
            nc.vector.tensor_scalar(value_scale[:, :], vec[:, 7:8], D ** 0.5 / CTX_UP, None, ALU.mult)
            chain.link(nc.vector.tensor_tensor(half_rz[:, :], vec[:, 0:2], vec[:, 3:5], ALU.add))
            nc.vector.tensor_scalar(half_rz[:, :], half_rz[:, :], 0.5, None, ALU.mult).then_inc(setup_copied, 1)
            dve.wait_ge(setup_mm, 2)
            nc.vector.tensor_scalar(wqk[:, :], score_ps[:, 0, 0:D], vec[:, 6:7], None, ALU.mult).then_inc(setup_copied, 1)
            dve.wait_ge(x_loaded, DMA)
            layernorm(x_in, RT)
            sum_squares(0, 0)
            dve.wait_ge(setup_mm, 3)
            nc.vector.tensor_copy(wih_t[:, :], score_ps[:, 1, 0:3 * D]).then_inc(setup_copied, 1)
            dve.wait_ge(setup_mm, 4)
            nc.vector.tensor_copy(wh_t[:, :], score_ps[:, 2, 0:3 * D]).then_inc(setup_copied, 1)
            dve.wait_ge(setup_mm, 5)
            nc.vector.tensor_copy(router_t[:, :], score_ps[:, 3, 0:EXPERTS]).then_inc(setup_copied, 1)
            dve.wait_ge(setup_mm, 6)
            nc.vector.tensor_scalar(wx_t[:, :], score_ps[:, 0, 0:3 * D], value_scale[:, :], None, ALU.mult)\
                .then_inc(setup_copied, 1)
            for e in range(PREP):
                if e >= 3:
                    copy_turned(0, e - 3)
                if 1 <= e < PAIR:
                    sum_squares(0, e)
                for t in (2 * e, 2 * e + 1):
                    if t < 2 * WTILES:
                        dve.wait_ge(wtile_hi, t + 1)
                        w = w1_t if t < WTILES else w2_t
                        nc.vector.scalar_tensor_tensor(out=w[:, LO, t % WTILES, :], in0=score_ps[:, t % 4, :], scalar=W_UP,
                                                       in1=w[:, HI, t % WTILES, :], op0=ALU.mult, op1=ALU.subtract)\
                            .then_inc(wtile_copied, 1)
                if 1 <= e <= PAIR:
                    rows_lo(0, e - 1)

            def wide(a):
                return a.unsqueeze(2).to_broadcast([ROWS, RT, EXPERTS])

            def router_probs(i):
                logits = gru_ps[0:ROWS, 0, 0:RT * EXPERTS].rearrange("p (t e) -> p t e", e=EXPERTS)
                wait(dve, logits_ready, nth(i, 1, 1))
                chain.link(nc.vector.tensor_reduce(rs_m[:], logits, AX_X, ALU.max))
                nc.vector.tensor_tensor(rs_z[:], logits, wide(rs_m[:]), ALU.subtract).then_inc(router_shift, 1)
                wait(dve, router_exp, nth(i, 1, 1))
                chain.link(nc.vector.tensor_reduce(rs_m[:], rs_e[:], AX_X, ALU.add))
                chain.link(nc.vector.reciprocal(rs_m[:], rs_m[:]))
                chain.link(nc.vector.tensor_tensor(rs_p[:], rs_e[:], wide(rs_m[:]), ALU.mult))

            def largest(src, dst):
                chain.link(nc.vector.tensor_reduce(rs_m[:], src[:], AX_X, ALU.max))
                chain.link(nc.vector.tensor_tensor(rs_k[:], src[:], wide(rs_m[:]), ALU.is_equal))
                chain.link(nc.vector.tensor_tensor(rs_k[:], rs_k[:], rank[:], ALU.mult))
                chain.link(nc.vector.tensor_reduce(rs_m[:], rs_k[:], AX_X, ALU.max))
                chain.link(nc.vector.tensor_tensor(dst[:], rs_k[:], wide(rs_m[:]), ALU.is_equal))

            def second_largest():
                chain.link(nc.vector.scalar_tensor_tensor(out=rs_q[:], in0=rs_1[:], scalar=-2.0, in1=rs_p[:],
                                                          op0=ALU.mult, op1=ALU.add))
                largest(rs_q, rs_z)

            def mix_weights():
                chain.link(nc.vector.tensor_tensor(mix[:], rs_1[:], rs_z[:], ALU.add))
                chain.link(nc.vector.scalar_tensor_tensor(out=mix[:], in0=mix[:], scalar=1.0 / W_UP, in1=rs_p[:],
                                                          op0=ALU.mult, op1=ALU.mult))

            place_rstd(0, 0)
            scale_qk(0, 0)
            qk_lo(0, 0)

            def body(i, more):
                chain.enter(PRO + i * PER)
                for n in range(ROUNDS):
                    gs, done, m, s = gates_at(n), slots_at(n), queries_at(n), n - 1
                    if n < STEPS:
                        banks = score_ps[0:TP, 2 * (n % 2):2 * (n % 2) + 2, 0:HALF * SLOTS]\
                            .rearrange("p h (c k) -> p h c k", k=SLOTS)
                        wait(dve, scores_ready, nth(i, STEPS, n + 1))
                        nc.vector.tensor_reduce(top[0:TP, n % 2], banks, AX_X, ALU.max).then_inc(max_ready, 1)
                    if queries_at(n - 1) is not None:
                        qk_lo(i, queries_at(n - 1))
                    if 0 <= s < STEPS:
                        wait(dve, exp_ready, nth(i, STEPS, s + 1))
                        nc.vector.tensor_reduce(den[0:TP, s % 2], soft[0:TP, s % 4], AX_X, ALU.add).then_inc(den_ready, 1)
                    if done is not None and tile_done_at(n - 1) is not None:
                        add_slots(i, tile_done_at(n - 1))
                    if done is not None:
                        wait(dve, ghn_ready, nth(i, GSTEPS, done + 1))
                        wait(dve, gates_tanh, nth(i, 2 * GSTEPS, 2 * done + 2))
                        nc.vector.scalar_tensor_tensor(out=npre[:, :], in0=gates[:, 0:GW], scalar=1.0, in1=gh_n[:, :],
                                                       op0=ALU.add, op1=ALU.mult).then_inc(r_ghn_ready, 1)
                        wait(dve, r_ghn_ready, nth(i, GSTEPS, done + 1))
                        nc.vector.tensor_tensor(npre[:, :], gru_ps[:, 0, 2 * GW:3 * GW], npre[:, :], ALU.add)\
                            .then_inc(npre_ready, 1)
                    if n < STEPS:
                        wait(dve, max_ready, nth(i, STEPS, n + 1))
                        wait_reuse(dve, attn_ready, i, STEPS, n - 3)
                        tops = top[0:TP, n % 2].rearrange("p (h c) -> p h c", h=2).unsqueeze(3)\
                            .to_broadcast([TP, 2, HALF, SLOTS])
                        nc.vector.tensor_tensor(soft[0:TP, n % 4].rearrange("p (h c) k -> p h c k", h=2), banks,
                                                tops, ALU.subtract).then_inc(shift_ready, 1)
                    if 0 <= s < STEPS:
                        wait(dve, den_ready, nth(i, STEPS, s + 1))
                        nc.vector.tensor_scalar(den[0:TP, s % 2], den[0:TP, s % 2], 1.0 / ATTN_UP, None, ALU.mult)\
                            .then_inc(den_scaled, 1)
                    if done is not None:
                        wait(dve, cand_ready, nth(i, GSTEPS, done + 1))
                        nc.vector.tensor_tensor(z_rest[:, :], z_rest[:, :], cand[:, :], ALU.mult).then_inc(cand_scaled, 1)
                    if m is not None:
                        place_rstd(i, m)
                    if 0 <= s < STEPS:
                        wait(dve, den_scaled, nth(i, STEPS, s + 1))
                        wait_reuse(dve, soft_ready, i, STEPS, s - 1)
                        nc.vector.reciprocal(rden[0:TP, s % 2], den[0:TP, s % 2]).then_inc(rden_ready, 1)
                    if done is not None:
                        wait(dve, cand_scaled, nth(i, GSTEPS, done + 1))
                        wait(dve, zh_ready, nth(i, GSTEPS, done + 1))
                        nc.vector.tensor_tensor(h[:, done % NG, :], z_rest[:, :], zh[:, :], ALU.add).then_inc(h_ready, 1)
                    if gs is not None:
                        wait(dve, upd_ready, nth(i, STEPS, GROUP * (gs + 1)))
                        nc.vector.reciprocal(inv_sum[:, :], upd_ps[:, gs % 2, GW:2 * GW]).then_inc(inv_ready, 1)
                    if m is not None:
                        scale_qk(i, m)
                    if gs is not None:
                        wait(dve, inv_ready, nth(i, GSTEPS, gs + 1))
                        nc.vector.tensor_tensor(upd[:, :], upd_ps[:, gs % 2, 0:GW], inv_sum[:, :], ALU.mult)\
                            .then_inc(upd_normed, 1)
                    if n >= STEPS and tile_done_at(n) is not None:
                        norm_tile(i, tile_done_at(n) - 1)
                    if more and early_at(n) is not None:
                        sum_squares(i + 1, early_at(n))
                add_slots(i, RT - 1)
                norm_tile(i, RT - 2)
                norm_tile(i, RT - 1)
                wait(dve, y_hi_ready, nth(i, 1, 1))
                wait(dve, cols_ready, nth(i, LN_PER, 2))
                nc.vector.tensor_tensor(ycols16[:, LO, :], ycols[:, :], ycols16[:, HI, :], ALU.subtract)\
                    .then_inc(y_split, 1)
                router_probs(i)
                for n in range(CH + HC):
                    e, c = divmod(n, HC)
                    if 1 <= n <= CH:
                        k = n - 1
                        wait(dve, hid_hi_ready, nth(i, CH, k + 1))
                        nc.vector.tensor_tensor(hidden[:, k % HRING, LO, 0:PW], hid32[:, k % GRING, :],
                                                hidden[:, k % HRING, HI, 0:PW], ALU.subtract).then_inc(hid_ready, 1)
                    if n == 1:
                        largest(rs_p, rs_1)
                    if n == 2:
                        second_largest()
                    if n == 3:
                        mix_weights()
                    if e >= 1 and c == 2:
                        wait(dve, down_ready, nth(i, CH, HC * e))
                        if e >= 2:
                            wait(dve, mixed, nth(i, EXPERTS, e - 1))
                        for t in range(RT):
                            ins = nc.vector.scalar_tensor_tensor(
                                out=acc[:, t, :], in0=score_ps[0:ROWS, 2 + (e - 1) % 2, t * D:(t + 1) * D],
                                scalar=mix[:, t, e - 1:e], in1=acc[:, t, :], op0=ALU.mult, op1=ALU.add)
                        ins.then_inc(mixed, 1)
                    if more:
                        if EARLY <= e + 1 < PAIR and c == 1:
                            sum_squares(i + 1, e + 1)
                        if e < PAIR and c == (3 if e < PAIR - 1 else 2):
                            rows_lo(i + 1, e)
                        if 1 <= e and c == 1:
                            copy_turned(i + 1, e - 1)
                        if n == 3 * HC + 3:
                            wait(dve, x_loaded, nth(i + 1, DMA, DMA))
                            layernorm(x_in, nth(i + 1, LNT_PER, RT))
                        if n == SPREAD_AT - 1:
                            place_rstd(i + 1, 0)
                        if n == SPREAD_AT + 1:
                            scale_qk(i + 1, 0)
                        if n == SPREAD_AT + 4:
                            qk_lo(i + 1, 0)

            with dve.Fori(0, NPAIR - 1) as i:
                body(i, True)
            body(NPAIR - 1, False)


_INS = ['x', 'ctx_1024', 'L0_xattn_Wq', 'L0_xattn_Wk', 'L0_xattn_Wv', 'L0_xattn_gru_wih', 'L0_xattn_gru_whh',
        'L0_xattn_gru_bih', 'L0_xattn_gru_bhh', 'L0_xattn_slot_norm_w', 'L0_xattn_input_norm_w',
        'L0_ffn_router_w', 'L0_ffn_w1', 'L0_ffn_w2']
_OUT = ((32, 56, 128), 'float32')


def kernel(**inputs):
    import numpy as _np
    import concourse.bacc as _bacc
    from concourse import mybir as _mybir
    from concourse.bass_utils import run_bass_kernel_spmd as _run

    nc = _bacc.Bacc("TRN2", target_bir_lowering=False, num_devices=1)
    arrays, args = {}, []
    for name in _INS:
        a = _np.ascontiguousarray(inputs[name])
        arrays[f"in_{name}_dram"] = a
        args.append(nc.dram_tensor(f"in_{name}_dram", a.shape, _mybir.dt.from_np(a.dtype), kind="ExternalInput").ap())
    dt = _mybir.dt.from_np(_np.dtype(_OUT[1]))
    args.append(nc.dram_tensor("out_0_dram", _OUT[0], dt, kind="ExternalOutput").ap())
    slot_attention_moe(nc, *args)
    r = _run(nc, [arrays], core_ids=[0])
    return r.results[0]["out_0_dram"]
```
